# Optimizing a Trainium2 kernel written in Bass

```python
import numpy as np
import jax
import jax.numpy as jnp

def _softmax(x, axis=-1):
    return jax.nn.softmax(x, axis=axis)

def _gelu(x):
    return jax.nn.gelu(x, approximate=True)

def _silu(x):
    return jax.nn.silu(x)

def _sigmoid(x):
    return jax.nn.sigmoid(x)

def _layernorm(x, axis=-1, eps=1e-05):
    m = jnp.mean(x, axis=axis, keepdims=True)
    v = jnp.var(x, axis=axis, keepdims=True)
    return (x - m) / jnp.sqrt(v + eps)

def _scatter_add(tgt, idx, src, axis=0):
    return tgt.at[idx].add(src)

def _segment_sum(src, seg, n):
    return jax.ops.segment_sum(src, seg, n)
kernel_name = 'mk_seq_postln_d1_jaxref_r4_50937c'

def setup_inputs(seed: int=0):
    np.random.seed(seed)
    _w = jnp.asarray

    def _L0_attn_setup():
        import jax, jax.numpy as jnp
        import numpy as np
        D_MODEL, N_HEADS = (256, 16)
        D_H = D_MODEL // N_HEADS
        D_HR = D_H // 2
        D_LATENT = 64
        THETA = 10000.0

        def rope(x, theta=THETA):
            S, d = (x.shape[-2], x.shape[-1])
            inv = theta ** (-jnp.arange(0, d, 2, dtype=jnp.float32) / d)
            ang = jnp.arange(S, dtype=jnp.float32)[:, None] * inv
            cos, sin = (jnp.cos(ang), jnp.sin(ang))
            x1, x2 = (x[..., 0::2], x[..., 1::2])
            r1 = x1 * cos - x2 * sin
            r2 = x1 * sin + x2 * cos
            return jnp.stack([r1, r2], axis=-1).reshape(x.shape)
        key = jax.random.key(seed)
        ks = jax.random.split(key, 9)
        s = lambda fan_in: 1.0 / np.sqrt(fan_in)
        return {'x': jax.random.normal(ks[0], (4, 512, D_MODEL), jnp.float32), 'W_DQ': jax.random.normal(ks[1], (D_MODEL, D_LATENT), jnp.float32) * s(D_MODEL), 'W_UQ': jax.random.normal(ks[2], (D_LATENT, N_HEADS * D_H), jnp.float32) * s(D_LATENT), 'W_QR': jax.random.normal(ks[3], (D_LATENT, N_HEADS * D_HR), jnp.float32) * s(D_LATENT), 'W_DKV': jax.random.normal(ks[4], (D_MODEL, D_LATENT), jnp.float32) * s(D_MODEL), 'W_UK': jax.random.normal(ks[5], (D_LATENT, N_HEADS * D_H), jnp.float32) * s(D_LATENT), 'W_UV': jax.random.normal(ks[6], (D_LATENT, N_HEADS * D_H), jnp.float32) * s(D_LATENT), 'W_KR': jax.random.normal(ks[7], (D_MODEL, D_HR), jnp.float32) * s(D_MODEL), 'W_O': jax.random.normal(ks[8], (N_HEADS * D_H, D_MODEL), jnp.float32) * s(N_HEADS * D_H)}
    _L0_attn_in = _L0_attn_setup()

    def _L0_ffn_setup():
        import jax, jax.numpy as jnp
        import numpy as np
        B, S, DIM = (4, 512, 256)
        E, K, HID = (8, 2, 1024)
        key = jax.random.key(seed)
        ks = jax.random.split(key, 8)
        init = lambda k, sh: jax.random.normal(k, sh, jnp.float32) * 0.02
        return {'x': jax.random.normal(ks[0], (B, S, DIM), jnp.float32), 'gate_w': init(ks[1], (DIM, E)), 'gate_b': jnp.zeros((E,), jnp.float32), 'w1': init(ks[2], (E, DIM, HID)), 'b1': jnp.zeros((E, HID), jnp.float32), 'w2': init(ks[3], (E, HID, DIM)), 'b2': jnp.zeros((E, DIM), jnp.float32), 'ws1': init(ks[4], (DIM, HID)), 'bs1': jnp.zeros((HID,), jnp.float32), 'ws2': init(ks[5], (HID, DIM)), 'bs2': jnp.zeros((DIM,), jnp.float32)}
    _L0_ffn_in = _L0_ffn_setup()
    _d = {'L0_attn_x': _L0_attn_in['x'], 'L0_attn_W_DQ': _L0_attn_in['W_DQ'], 'L0_attn_W_UQ': _L0_attn_in['W_UQ'], 'L0_attn_W_QR': _L0_attn_in['W_QR'], 'L0_attn_W_DKV': _L0_attn_in['W_DKV'], 'L0_attn_W_UK': _L0_attn_in['W_UK'], 'L0_attn_W_UV': _L0_attn_in['W_UV'], 'L0_attn_W_KR': _L0_attn_in['W_KR'], 'L0_attn_W_O': _L0_attn_in['W_O'], 'L0_ffn_gate_w': _L0_ffn_in['gate_w'], 'L0_ffn_gate_b': _L0_ffn_in['gate_b'], 'L0_ffn_w1': _L0_ffn_in['w1'], 'L0_ffn_b1': _L0_ffn_in['b1'], 'L0_ffn_w2': _L0_ffn_in['w2'], 'L0_ffn_b2': _L0_ffn_in['b2'], 'L0_ffn_ws1': _L0_ffn_in['ws1'], 'L0_ffn_bs1': _L0_ffn_in['bs1'], 'L0_ffn_ws2': _L0_ffn_in['ws2'], 'L0_ffn_bs2': _L0_ffn_in['bs2']}
    _x0 = _d['L0_attn_x']
    _d['L0_attn_x'] = jax.random.normal(jax.random.fold_in(jax.random.key(seed), 1), (8, 512, 256), dtype=_x0.dtype)
    del _x0
    return _d

def reference(L0_attn_x, L0_attn_W_DQ, L0_attn_W_UQ, L0_attn_W_QR, L0_attn_W_DKV, L0_attn_W_UK, L0_attn_W_UV, L0_attn_W_KR, L0_attn_W_O, L0_ffn_gate_w, L0_ffn_gate_b, L0_ffn_w1, L0_ffn_b1, L0_ffn_w2, L0_ffn_b2, L0_ffn_ws1, L0_ffn_bs1, L0_ffn_ws2, L0_ffn_bs2):

    def _L0_attn_ref(x, W_DQ, W_UQ, W_QR, W_DKV, W_UK, W_UV, W_KR, W_O):
        import jax, jax.numpy as jnp
        import numpy as np
        D_MODEL, N_HEADS = (256, 16)
        D_H = D_MODEL // N_HEADS
        D_HR = D_H // 2
        D_LATENT = 64
        THETA = 10000.0

        def rope(x, theta=THETA):
            S, d = (x.shape[-2], x.shape[-1])
            inv = theta ** (-jnp.arange(0, d, 2, dtype=jnp.float32) / d)
            ang = jnp.arange(S, dtype=jnp.float32)[:, None] * inv
            cos, sin = (jnp.cos(ang), jnp.sin(ang))
            x1, x2 = (x[..., 0::2], x[..., 1::2])
            r1 = x1 * cos - x2 * sin
            r2 = x1 * sin + x2 * cos
            return jnp.stack([r1, r2], axis=-1).reshape(x.shape)
        B, S, _ = x.shape
        d_qk = D_H + D_HR
        c_q = x @ W_DQ
        Qc = (c_q @ W_UQ).reshape(B, S, N_HEADS, D_H).transpose(0, 2, 1, 3)
        Qr = (c_q @ W_QR).reshape(B, S, N_HEADS, D_HR).transpose(0, 2, 1, 3)
        Qr = rope(Qr)
        c_kv = x @ W_DKV
        Kc = (c_kv @ W_UK).reshape(B, S, N_HEADS, D_H).transpose(0, 2, 1, 3)
        Kr = rope((x @ W_KR)[:, None, :, :])
        Kr = jnp.broadcast_to(Kr, (B, N_HEADS, S, D_HR))
        V = (c_kv @ W_UV).reshape(B, S, N_HEADS, D_H).transpose(0, 2, 1, 3)
        Q = jnp.concatenate([Qc, Qr], axis=-1)
        K = jnp.concatenate([Kc, Kr], axis=-1)
        scores = jnp.einsum('bhqd,bhkd->bhqk', Q, K)
        scores = jnp.clip(scores, -80.0, 80.0)
        causal = jnp.tril(jnp.ones((S, S), dtype=bool))
        scores = jnp.where(causal, scores, -jnp.inf)
        weights = jax.nn.softmax(scores / jnp.sqrt(jnp.float32(d_qk)), axis=-1)
        attn = jnp.einsum('bhqk,bhkd->bhqd', weights, V)
        attn = attn.transpose(0, 2, 1, 3).reshape(B, S, N_HEADS * D_H)
        return attn @ W_O

    def _L0_ffn_ref(x, gate_w, gate_b, w1, b1, w2, b2, ws1, bs1, ws2, bs2):
        import jax, jax.numpy as jnp
        import numpy as np
        B, S, DIM = (4, 512, 256)
        E, K, HID = (8, 2, 1024)
        orig_shape = x.shape
        xf = x.reshape(-1, DIM)
        logits = xf @ gate_w + gate_b
        top_w, top_i = jax.lax.top_k(logits, K)
        gw = jax.nn.softmax(top_w, axis=-1).astype(xf.dtype)
        combine = (gw[:, :, None] * jax.nn.one_hot(top_i, E, dtype=xf.dtype)).sum(axis=1)
        out = jnp.zeros_like(xf)
        for e in range(E):
            h = jax.nn.gelu(xf @ w1[e] + b1[e], approximate=False)
            out = out + combine[:, e:e + 1] * (h @ w2[e] + b2[e])
        shared = jax.nn.gelu(xf @ ws1 + bs1, approximate=False) @ ws2 + bs2
        return (out + shared).reshape(orig_shape)
    x = L0_attn_x
    x = _layernorm(x + _L0_attn_ref(x, L0_attn_W_DQ, L0_attn_W_UQ, L0_attn_W_QR, L0_attn_W_DKV, L0_attn_W_UK, L0_attn_W_UV, L0_attn_W_KR, L0_attn_W_O), axis=-1)
    x = _layernorm(x + _L0_ffn_ref(x, L0_ffn_gate_w, L0_ffn_gate_b, L0_ffn_w1, L0_ffn_b1, L0_ffn_w2, L0_ffn_b2, L0_ffn_ws1, L0_ffn_bs1, L0_ffn_ws2, L0_ffn_bs2), axis=-1)
    return x

_drawn_inputs = setup_inputs


def setup_inputs(seed=0):
    import zlib

    import numpy as np

    out = dict(_drawn_inputs(seed))
    spreads = {'L0_ffn_gate_b': (0.0, 0.1),
     'L0_ffn_b1': (0.0, 0.311),
     'L0_ffn_b2': (0.0, 0.1),
     'L0_ffn_bs1': (0.0, 0.1),
     'L0_ffn_bs2': (0.0, 0.1)}
    factors = {}
    for name, (base, spread) in spreads.items():
        noise = np.random.default_rng([zlib.crc32(name.encode()), seed]).standard_normal(out[name].shape)
        drawn = base * np.exp(spread * noise) if base else spread * noise
        out[name] = jnp.asarray(drawn.astype(out[name].dtype))
    for name, factor in factors.items():
        out[name] = (out[name] * factor).astype(out[name].dtype)
    return out
```

```python
from contextlib import ExitStack

import numpy as np
import concourse.bass as bass
from concourse import mybir

F32 = mybir.dt.float32
F32R = mybir.dt.float32r
I32 = mybir.dt.int32
ALU = mybir.AluOpType
ACT = mybir.ActivationFunctionType
AX_X = mybir.AxisListType.X

P = 128
B, S, D = 8, 512, 256
T = B * S
NT = T // P
H, DH, DR = 16, 16, 8
LAT = 64
SLOT = 32
HG = P // SLOT
G = H // HG
KB = S // P
DC = D // P
SCALE = 1.0 / float(np.sqrt(np.float32(DH + DR)))
E, HID = 8, 1024
TOP = 2
TS = 512
TILES = TOP * T // TS + E - 1
SLOTS = TILES * TS
CLIP = 80.0
EPS = 1e-5

COLS = [S - P * j for j in range(KB)]
AT = [0, S, 2 * S, S + COLS[1]]
EW = sum(COLS)


def attention(nc, x, xT, w_down, w_q, w_kv, w_kr, w_o, rope, masks, res, slots_in):
    with ExitStack() as ctx:
        def sb(name, shape, dt=F32):
            return ctx.enter_context(nc.sbuf_tensor(name, shape, dt))

        def sem(name):
            return ctx.enter_context(nc.semaphore(name))

        xt = sb("xt", [P, DC, T])
        wd = sb("wd", [P, DC, 2 * LAT])
        wq = sb("wq", [LAT, G, 2, P])
        wkv = sb("wkv", [P, G * P + D])
        wkr = sb("wkr", [P, DC, 2, P])
        wo = sb("wo", [P, G, D])
        cs = sb("cs", [P, 2, S])
        mk = sb("mk", [P, P])
        cT = sb("cT", [P, S])
        kr = sb("kr", [P, S])
        sinpart = sb("sinpart", [P, 2, S])
        qt = sb("qt", [P, G, S])
        kt = sb("kt", [P, G, S])
        v = sb("v", [P, KB, H, SLOT])
        e = sb("e", [P, 4, EW])
        ot = sb("ot", [P, 2, S])
        rec = sb("rec", [P, 2, S])
        on = sb("on", [P, G, S])
        bn = sb("bn", [P, KB, 6])
        mv = sb("mv", [P, KB, 2])
        var = sb("var", [P, KB])
        rstd = sb("rstd", [P, KB])
        minus_half = sb("minus_half", [P, KB])
        row = sb("row", [P, KB, D])
        causal = sb("causal", [P, 2, P])
        zeros = sb("zeros", [P, TS // P * D])
        ps = ctx.enter_context(nc.psum_tensor("ps", [P, 8, S], F32))

        consts_in = sem("consts_in")
        x_in = sem("x_in")
        ones_set = sem("ones_set")
        c_ready, ct_done = sem("c_ready"), sem("ct_done")
        kr_ready, kr_steps = sem("kr_ready"), sem("kr_steps")
        v_ready, v_done = sem("v_ready"), sem("v_done")
        qk_ready, rope_steps, q_done = sem("qk_ready"), sem("rope_steps"), sem("q_done")
        s_ready, exp_done, clip_done, mask_done = sem("s_ready"), sem("exp_done"), sem("clip_done"), sem("mask_done")
        pv_done, ot_done, sum_ready, rec_done, on_done = sem("pv_done"), sem("ot_done"), sem("sum_ready"), sem("rec_done"), sem("on_done")
        a_ready, res_done, bn_done, mv_done = sem("a_ready"), sem("res_done"), sem("bn_done"), sem("mv_done")
        var_done, rstd_done = sem("var_done"), sem("rstd_done")
        zeros_set, slots_zeroed = sem("zeros_set"), sem("slots_zeroed")

        block = ctx.enter_context(nc.Block())
        CONSTS = 9

        @block.sync
        def _(sp):
            for dst, src in ((wd, w_down), (wkr, w_kr), (cs, rope)):
                sp.dma_start(dst[:], src).then_inc(consts_in, 16)
            sp.dma_start(wq[:], w_q).then_inc(consts_in, 16)
            sp.dma_start(wkv[LAT:P, :], w_kv).then_inc(consts_in, 16)
            sp.dma_start(wo[:], w_o).then_inc(consts_in, 16)
            sp.dma_start(mk[:], masks[:, 0, :]).then_inc(consts_in, 16)
            for n in range(2):
                sp.dma_start(causal[:, n, :], masks[:, 4, :]).then_inc(consts_in, 16)
            sp.dma_start(xt[:, :, 0:S], xT[:, :, 0:S]).then_inc(x_in, 16)
            sp.dma_start(res[:, 0:KB, :], x[:, 0:KB, :]).then_inc(x_in, 16)
            with sp.Fori(1, B) as b:
                sp.wait_ge(x_in, 32 * b)
                sp.dma_start(xt[:, :, bass.ds(b * S, S)],
                             xT[:, :, bass.ds(b * S, S)]).then_inc(x_in, 16)
                sp.dma_start(res[:, bass.ds(b * KB, KB), :],
                             x[:, bass.ds(b * KB, KB), :]).then_inc(x_in, 16)
            sp.wait_ge(x_in, 32 * B)
            sp.wait_ge(zeros_set, 1)
            with sp.Fori(0, TILES) as n:
                sp.dma_start(slots_in[bass.ds(n * TS, TS), :].rearrange("(p c) d -> p (c d)", p=P),
                             zeros[:, :]).then_inc(slots_zeroed, 16)
            sp.wait_ge(slots_zeroed, 16 * TILES)

        @block.tensor
        def _(pe):
            pe.wait_ge(consts_in, 16 * CONSTS)
            pe.wait_ge(ones_set, 1)
            with pe.Fori(0, B) as b:
                xb = xt[:, :, bass.ds(b * S, S)]
                pe.wait_ge(x_in, 32 * b + 32)
                for k in range(DC):
                    mm = pe.matmul(ps[:, 0, :], wd[:, k, :], xb[:, k, :], start=k == 0, stop=k == DC - 1)
                mm.then_inc(c_ready, 1)
                for r in range(2):
                    for k in range(DC):
                        mm = pe.matmul(ps[:, 1 + r, :], wkr[:, k, r, :], xb[:, k, :], start=k == 0, stop=k == DC - 1)
                mm.then_inc(kr_ready, 1)
                pe.wait_ge(ct_done, b + 1)
                pe.wait_ge(kr_steps, 3 * b + 2)
                for t in range(KB):
                    mm = pe.matmul(ps[:, 3 + t // 2, (t % 2) * D:(t % 2) * D + D], cT[LAT:P, t * P:(t + 1) * P],
                                   wkv[LAT:P, G * P:], start=True, stop=True)
                    if t % 2:
                        mm.then_inc(v_ready, 1)
                for g in range(G):
                    bank = 3 * (g % 2)
                    if g == 1:
                        pe.wait_ge(v_done, 2 * b + 2)
                    if g >= 2:
                        pe.wait_ge(rope_steps, 12 * b + 3 * (g - 1))
                    pe.matmul(ps[:, bank, :], wq[:, g, 0, :], cT[0:LAT, :], start=True, stop=True)
                    pe.matmul(ps[:, bank + 1, :], wq[:, g, 1, :], cT[0:LAT, :], start=True, stop=True)
                    pe.matmul(ps[:, bank + 2, :], wkv[LAT:P, g * P:(g + 1) * P], cT[LAT:P, :],
                              start=True, stop=True).then_inc(qk_ready, 1)

                def scores(h):
                    g, i = h // HG, h % HG
                    if i == 0:
                        pe.wait_ge(q_done, G * b + g + 1)
                        pe.wait_ge(rope_steps, 12 * b + 3 * g + 3)
                    if h < 2:
                        pe.wait_ge(rope_steps, 12 * b + 12 - 3 * (1 - h))
                    else:
                        pe.wait_ge(exp_done, H * b + h - 1)
                    rows = slice(SLOT * i, SLOT * (i + 1))
                    for j in range(KB):
                        bank, col = 3 * (h % 2) + AT[j] // S, AT[j] % S
                        mm = pe.matmul(ps[:, bank, col:col + COLS[j]], kt[rows, g, P * j:P * (j + 1)],
                                       qt[rows, g, P * j:], start=True, stop=True)
                    mm.then_inc(s_ready, 1)

                def weigh(h):
                    g, i = h // HG, h % HG
                    if i == 0 and g >= 2:
                        pe.wait_ge(rec_done, G * b + g - 1)
                    pe.wait_ge(mask_done, H * b + h + 1)
                    for j in range(KB):
                        mm = pe.matmul(ps[SLOT * i:SLOT * (i + 1), 6 + g % 2, P * j:], v[:, j, h, :],
                                       e[:, h % 4, AT[j]:AT[j] + COLS[j]], start=j == 0, stop=j == KB - 1)
                    mm.then_inc(pv_done, 1)

                def sums(g):
                    pe.wait_ge(ot_done, G * b + g + 1)
                    pe.matmul(ps[:, 6 + g % 2, :], mk[:, :], ot[:, g % 2, :], start=True, stop=True).then_inc(sum_ready, 1)

                scores(0)
                for h in range(H):
                    if h + 1 < H:
                        scores(h + 1)
                    weigh(h)
                    if h % HG == 0 and h:
                        sums(h // HG - 1)
                sums(G - 1)
                pe.wait_ge(on_done, G * b + G)
                for t in range(KB):
                    for g in range(G):
                        mm = pe.matmul(ps[:, 3 + t // 2, (t % 2) * D:(t % 2) * D + D], on[:, g, t * P:(t + 1) * P],
                                       wo[:, g, :], start=g == 0, stop=g == G - 1)
                    if t % 2:
                        mm.then_inc(a_ready, 1)

        @block.scalar
        def _(act):
            with act.Fori(0, B) as b:
                act.wait_ge(c_ready, b + 1)
                act.activation(cT[:, :], ps[:, 0, :], ACT.Copy).then_inc(ct_done, 1)
                for n in range(2):
                    act.wait_ge(v_ready, 2 * b + n + 1)
                    act.activation(v[:, 2 * n:2 * n + 2, :, 0:DH],
                                   ps[:, 3 + n, :].rearrange("p (t h d) -> p t h d", t=2, h=H),
                                   ACT.Copy).then_inc(v_done, 1)
                for h in range(H):
                    act.wait_ge(s_ready, H * b + h + 1)
                    if h >= 4:
                        act.wait_ge(pv_done, H * b + h - 3)
                    bank = 3 * (h % 2)
                    act.activation(e[:, h % 4, 0:2 * S], ps[:, bank:bank + 2, :].rearrange("p a s -> p (a s)"),
                                   ACT.Exp, scale=SCALE)
                    act.activation(e[:, h % 4, 2 * S:EW], ps[:, bank + 2, 0:COLS[2]], ACT.Exp,
                                   scale=SCALE).then_inc(exp_done, 1)
                    if (h % HG == 0 and h) or h == H - 1:
                        g = (h - 1) // HG
                        act.wait_ge(pv_done, H * b + HG * (g + 1))
                        if g >= 2:
                            act.wait_ge(on_done, G * b + g - 1)
                        act.activation(ot[:, g % 2, :], ps[:, 6 + g % 2, :], ACT.Copy).then_inc(ot_done, 1)

        @block.gpsimd
        def _(pool):
            pool.memset(v[:, :, :, DH:], 1.0).then_inc(ones_set, 1)
            pool.memset(minus_half[:, :], -0.5)
            pool.memset(zeros[:, :], 0.0).then_inc(zeros_set, 1)
            pool.wait_ge(consts_in, 16 * CONSTS)
            with pool.Fori(0, B) as b:
                for g in range(G):
                    pool.wait_ge(rope_steps, 12 * b + 3 * g + 2)
                    pool.tensor_tensor(qt[:, g, :], qt[:, g, :], sinpart[:, g % 2, :], ALU.add).then_inc(q_done, 1)
                for h in range(H):
                    pool.wait_ge(clip_done, H * b + h + 1)
                    a = e[:, h % 4, 0:2 * S].rearrange("p (a s) -> p a s", a=2)[:, :, 0:P]
                    c = e[:, h % 4, AT[3]:AT[2] + P].rearrange("p (a s) -> p a s", a=2)
                    pool.tensor_tensor(a, a, causal[:, :, :], ALU.mult)
                    pool.tensor_tensor(c, c, causal[:, :, :], ALU.mult).then_inc(mask_done, 1)
                pool.wait_ge(var_done, b + 1)
                pool.tensor_tensor(rstd[:, :], var[:, :], minus_half[:, :], ALU.pow).then_inc(rstd_done, 1)

        @block.vector
        def _(dve):
            low, high = float(np.exp(-CLIP * SCALE)), float(np.exp(CLIP * SCALE))
            dve.wait_ge(consts_in, 16 * CONSTS)
            with dve.Fori(0, B) as b:
                dve.wait_ge(kr_ready, b + 1)
                dve.tensor_tensor(kr[:, :], ps[:, 1, :], cs[:, 0, :], ALU.mult).then_inc(kr_steps, 1)
                dve.tensor_tensor(sinpart[:, 0, :], ps[:, 2, :], cs[:, 1, :], ALU.mult).then_inc(kr_steps, 1)
                dve.wait_ge(kr_steps, 3 * b + 2)
                dve.tensor_tensor(kr[:, :], kr[:, :], sinpart[:, 0, :], ALU.add).then_inc(kr_steps, 1)
                dve.wait_ge(kr_steps, 3 * b + 3)
                for g in range(G):
                    bank = 3 * (g % 2)
                    dve.wait_ge(qk_ready, G * b + g + 1)
                    if g >= 2:
                        dve.wait_ge(q_done, G * b + g - 1)
                    dve.tensor_tensor(qt[:, g, :], ps[:, bank, :], cs[:, 0, :], ALU.mult).then_inc(rope_steps, 1)
                    dve.tensor_tensor(sinpart[:, g % 2, :], ps[:, bank + 1, :], cs[:, 1, :], ALU.mult).then_inc(rope_steps, 1)
                    dve.tensor_tensor(kt[:, g, :], ps[:, bank + 2, :], kr[:, :], ALU.add).then_inc(rope_steps, 1)

                def norm(g):
                    dve.wait_ge(sum_ready, G * b + g + 1)
                    dve.reciprocal(rec[:, g % 2, :], ps[:, 6 + g % 2, :]).then_inc(rec_done, 1)
                    dve.wait_ge(rec_done, G * b + g + 1)
                    dve.tensor_tensor(on[:, g, :], ot[:, g % 2, :], rec[:, g % 2, :], ALU.mult).then_inc(on_done, 1)

                for h in range(H):
                    dve.wait_ge(exp_done, H * b + h + 1)
                    dve.tensor_scalar(e[:, h % 4, :], e[:, h % 4, :], high, low, ALU.min, ALU.max).then_inc(clip_done, 1)
                    if h % HG == 1 and h > HG:
                        norm(h // HG - 1)
                norm(G - 1)
                for t in range(KB):
                    if t % 2 == 0:
                        dve.wait_ge(a_ready, 2 * b + t // 2 + 1)
                    dve.tensor_tensor(row[:, t, :], ps[:, 3 + t // 2, (t % 2) * D:(t % 2) * D + D],
                                      res[:, bass.ds(b * KB + t, 1), :].rearrange("p a d -> p (a d)"),
                                      ALU.add).then_inc(res_done, 1)
                    dve.wait_ge(res_done, KB * b + t + 1)
                    dve.bn_stats(bn[:, t, :], row[:, t, :]).then_inc(bn_done, 1)
                dve.wait_ge(consts_in, 16 * CONSTS)
                dve.wait_ge(bn_done, KB * b + KB)
                for t in range(KB):
                    dve.bn_aggr(mv[:, t, :], bn[:, t, :]).then_inc(mv_done, 1)
                dve.wait_ge(mv_done, KB * (b + 1))
                dve.tensor_scalar(var[:, :], mv[:, :, 1], EPS, None, ALU.add).then_inc(var_done, 1)
                dve.wait_ge(rstd_done, b + 1)
                for t in range(KB):
                    dve.tensor_scalar(res[:, bass.ds(b * KB + t, 1), :].rearrange("p a d -> p (a d)"), row[:, t, :],
                                      mv[:, t, 0:1], rstd[:, t:t + 1], ALU.subtract, ALU.mult)


def experts(nc, res, slots_in, slots_out, w1, w2, b1, b2, gate_w, gate_b, masks, numbers, out):
    C = TS // P
    HC = HID // P
    HEAD = 4
    LAST = HEAD + TILES
    END = T // TS + TILES
    PIECE = DC * HID // HC * 2
    HALF = HC // 2
    with ExitStack() as ctx:
        def sb(name, shape, dt=F32):
            return ctx.enter_context(nc.sbuf_tensor(name, shape, dt))

        def sem(name):
            return ctx.enter_context(nc.semaphore(name))

        w1raw, w2raw = sb("w1raw", [P, DC, HID]), sb("w2raw", [P, HC, D])
        w1hi, w1lo = sb("w1hi", [P, 2, DC, HID], F32R), sb("w1lo", [P, 2, DC, HID], F32R)
        w2hi, w2lo = sb("w2hi", [P, 2, HC, D], F32R), sb("w2lo", [P, 2, HC, D], F32R)
        bias1, bias2 = sb("bias1", [P, 2, HC]), sb("bias2", [P, 2, D])
        rows = sb("rows", [P, 2, C, D])
        xhi, xlo = sb("xhi", [P, 2, DC, TS], F32R), sb("xlo", [P, 2, DC, TS], F32R)
        yT = sb("yT", [P, 2, DC, TS])
        h = sb("h", [P, 2, TS])
        hhi, hlo = sb("hhi", [P, 2, TS], F32R), sb("hlo", [P, 2, TS], F32R)
        ys = sb("ys", [P, 2, C, D])
        ident, before, ones = sb("ident", [P, P]), sb("before", [P, P]), sb("ones", [P, P])
        nums = sb("nums", [P, E + TILES])
        gw, gb = sb("gw", [P, DC, E]), sb("gb", [P, E])
        logits = sb("logits", [P, NT, E])
        first, second, both = sb("first", [P, NT, E]), sb("second", [P, NT, E]), sb("both", [P, NT, E])
        work = sb("work", [P, NT, E])
        total, upto, zero = sb("total", [P, E, NT]), sb("upto", [P, E, NT]), sb("zero", [P, E * NT])
        best, pick, next_best = sb("best", [P, NT]), sb("pick", [P, NT]), sb("next_best", [P, NT])
        gap, den = sb("gap", [P, NT]), sb("den", [P, NT])
        wt = sb("wt", [P, TOP, NT])
        slotf, slot = sb("slotf", [P, TOP, NT]), sb("slot", [P, TOP, NT], I32)
        count, tiles_i, tiles_f = sb("count", [P, E]), sb("tiles_i", [P, E], I32), sb("tiles_f", [P, E])
        tiles_upto, base = sb("tiles_upto", [P, E]), sb("base", [P, E])
        passed, owner, owner_i = sb("passed", [P, TILES, E]), sb("owner", [P, TILES]), sb("owner_i", [P, TILES], I32)
        back = sb("back", [P, 4, TOP, D])
        bn, mv = sb("bn2", [P, 2, 6]), sb("mv2", [P, 2, 2])
        var, rstd, minus_half = sb("var2", [P, 2]), sb("rstd2", [P, 2]), sb("minus_half2", [P, 1])
        fin = sb("fin", [P, 4, D])
        ps = ctx.enter_context(nc.psum_tensor("ps2", [P, 8, 512], F32))

        consts_in, minus_set = sem("consts_in2"), sem("minus_set")
        gt_ready, gt_done, lg_ready, lg_done = sem("gt_ready"), sem("gt_done"), sem("lg_ready"), sem("lg_done")
        route_step, gap_done, gap_exp, both_done, ranks_ready, slots_known = (
            sem("route_step"), sem("gap_done"), sem("gap_exp"), sem("both_done"), sem("ranks_ready"), sem("slots_known"))
        sent = sem("sent")
        w1_in, w2_in, b_in, x_in = sem("w1_in"), sem("w2_in"), sem("b_in"), sem("x_in2")
        w_hi, w_lo = sem("w_hi"), sem("w_lo")
        tr_ready, xhi_done, xlo_done = sem("tr_ready"), sem("xhi_done"), sem("xlo_done")
        m1_ready, gelu_done, hhi_done, h_done = sem("m1_ready"), sem("gelu_done"), sem("hhi_done"), sem("h_done")
        y_ready, ysum, y_done, y_out = sem("y_ready"), sem("ysum"), sem("y_done"), sem("y_out")
        back_in = [sem(f"back_in{n}") for n in range(4)]
        c_step, var_done, rstd_done, fin_done = sem("c_step"), sem("var_done2"), sem("rstd_done2"), sem("fin_done")
        fin_out = [sem(f"fin_out{n}") for n in range(4)]

        block = ctx.enter_context(nc.Block())
        CONSTS = 6

        def slots_tile(dram, at):
            return dram.rearrange("s d -> (s d)")[bass.ds(at, TS * D)].rearrange("(p c d) -> p c d", p=P, c=C)


        def is_shared(s):
            return s < HEAD or s >= LAST

        def tokens(s):
            n = (s if s < HEAD else s - TILES) * C
            return range(n, n + C)

        LAG = 4
        LASTS = END - LAST

        @block.sync
        def _(sp):
            def load_w1(src):
                sp.dma_start(w1raw[:, :, :], src).then_inc(w1_in, 16)

            def load_w2(src):
                sp.dma_start(w2raw[:, :, :], src).then_inc(w2_in, 16)

            def load_b(e, u):
                sp.dma_start(bias1[:, u, :], b1[bass.ds(e, 1)].rearrange("e p c -> p (e c)")).then_inc(b_in, 16)
                sp.dma_start(bias2[:, u, :], b2[bass.ds(e, 1), :].to_broadcast([P, D])).then_inc(b_in, 16)

            def w1_of(e):
                return w1[bass.ds(e, 1)].rearrange("e (k p) n -> p (e k) n", p=P)

            def w2_of(e):
                return w2[bass.ds(e, 1)].rearrange("e (c p) n -> p (e c) n", p=P)

            load_w1(w1_of(E))
            load_w2(w2_of(E))
            load_b(E, 1)
            for dst, src in ((ident, masks[:, 1, :]), (before, masks[:, 2, :]), (ones, masks[:, 3, :]),
                             (nums, numbers), (gw, gate_w.rearrange("(k p) e -> p k e", p=P)),
                             (gb, gate_b.rearrange("(a e) -> a e", a=1).to_broadcast([P, E]))):
                sp.dma_start(dst[:], src).then_inc(consts_in, 16)

            def prefetch(s, u, shared_next=False):
                r = s + 1 - HEAD
                at = r * TS * D if isinstance(r, int) else sp.snap(r * (TS * D))
                e = E if shared_next else sp.value_load(owner_i[0:1, bass.ds(r, 1)], min_val=0, max_val=E - 1)
                sp.wait_ge(w_lo, HC * r + HALF)
                load_w1(w1_of(e))
                if not shared_next:
                    sp.wait_ge(x_in, 16 * r)
                    sp.wait_ge(tr_ready, 2 * s)
                    sp.dma_start(rows[:, 1 - u, :, :], slots_tile(slots_in, at)).then_inc(x_in, 16)
                sp.wait_ge(w_lo, HC * r + HC)
                load_w2(w2_of(e))
                sp.wait_ge(y_done, s)
                sp.wait_ge(b_in, 32 * (r + 1))
                load_b(e, 1 - u)
                return r

            def store(s, u):
                r = s - HEAD
                at = r * TS * D if isinstance(r, int) else sp.snap(r * (TS * D))
                sp.wait_ge(y_out, 16 * r + 32)
                sp.wait_ge(y_done, s + 1)
                sp.dma_start(slots_tile(slots_out, at), ys[:, u, :, :]).then_inc(y_out, 16)

            sp.sem_inc(y_out, 32)
            sp.wait_ge(slots_known, 1)
            e = sp.value_load(owner_i[0:1, 0:1], min_val=0, max_val=E - 1)
            sp.wait_ge(w_lo, HALF)
            load_w1(w1_of(e))
            sp.wait_ge(w_lo, HC)
            load_w2(w2_of(e))
            sp.wait_ge(b_in, 32)
            load_b(e, 0)
            sp.wait_ge(sent, 16 * TOP * NT)
            sp.dma_start(rows[:, 0, :, :], slots_tile(slots_in, 0)).then_inc(x_in, 16)
            prefetch(HEAD, 0)
            with sp.Fori(0, (TILES - 3) // 2) as i:
                for u in (1, 0):
                    s = HEAD + 2 * i + (1 if u else 2)
                    prefetch(s, u)
                    store(s - 1, 1 - u)
            prefetch(LAST - 2, 1)
            store(LAST - 3, 0)
            prefetch(LAST - 1, 0, shared_next=True)
            store(LAST - 2, 1)
            store(LAST - 1, 0)
            for t in range(NT):
                sp.wait_ge(fin_done, t + 1)
                sp.dma_start(out[t * P:(t + 1) * P, :], fin[:, t % 4, :]).then_inc(fin_out[t % 4], 16)
            for n in range(4):
                sp.wait_ge(fin_out[n], 16 * NT // 4)

        @block.tensor
        def _(pe):
            pe.wait_ge(consts_in, 16 * CONSTS)
            for q in range(NT // C):
                u = q % 2
                if q >= 2:
                    pe.wait_ge(gt_done, 2 * (q - 1))
                for k in range(DC):
                    for c in range(C):
                        mm = pe.transpose(ps[:, 2 * u + k, c * P:(c + 1) * P],
                                          res[:, C * q + c, k * P:(k + 1) * P], ident[:, :])
                    mm.then_inc(gt_ready, 1)
                pe.wait_ge(gt_done, 2 * (q + 1))
                if q >= 2:
                    pe.wait_ge(lg_done, q - 1)
                for c in range(C):
                    for k in range(DC):
                        mm = pe.matmul(ps[:, 4 + u, c * E:(c + 1) * E], yT[:, u, k, c * P:(c + 1) * P], gw[:, k, :],
                                       start=c == 0 and k == 0, stop=c == C - 1 and k == DC - 1, skip_group_check=True)
                mm.then_inc(lg_ready, 1)
            pe.wait_ge(both_done, 1)
            pe.matmul(ps[:, 0, 0:NT * E], before[:, :], both[:, :, :].rearrange("p t e -> p (t e)"), start=True, stop=True)
            pe.matmul(ps[:, 1, 0:NT * E], ones[:, :], both[:, :, :].rearrange("p t e -> p (t e)"),
                      start=True, stop=True).then_inc(ranks_ready, 1)

            def turn(s, u):
                if not is_shared_now:
                    pe.wait_ge(x_in, 16 * (s - HEAD + 1))
                for k in range(DC):
                    for c in range(C):
                        src = res[:, tokens(s)[c], :] if is_shared_now else rows[:, u, c, :]
                        mm = pe.transpose(ps[:, 6 + k, c * P:(c + 1) * P], src[:, k * P:(k + 1) * P], ident[:, :])
                    mm.then_inc(tr_ready, 1)

            def up(s, u, w, c, load=None):
                if c == 0:
                    pe.wait_ge(xhi_done, 2 * s + 2)
                    pe.wait_ge(xlo_done, 2 * s + 2)
                    if load is not None:
                        pe.wait_ge(w_lo, HC * load + HALF)
                cols = slice(c * P, (c + 1) * P)
                n = 0
                for k in range(DC):
                    for a, b in ((w1hi, xhi), (w1hi, xlo), (w1lo, xhi)):
                        mm = pe.matmul(ps[:, c % 2, :], a[:, w, k, cols], b[:, u, k, :], start=n == 0, stop=n == 3 * DC - 1)
                        n += 1
                mm.then_inc(m1_ready, 1)

            def down(s, u, w, c, load=None):
                if c == 0 and load is not None:
                    pe.wait_ge(w_lo, HC * load + HC)
                pe.wait_ge(h_done, HC * s + c + 1)
                for q in range(C):
                    to = ps[:, 2 + 2 * u + q // 2, (q % 2) * D:(q % 2) * D + D]
                    for n, (a, b) in enumerate(((hhi, w2hi), (hhi, w2lo), (hlo, w2hi))):
                        mm = pe.matmul(to, a[:, c % 2, q * P:(q + 1) * P], b[:, w, c, :],
                                       start=c == 0 and n == 0 and q % 2 == 0, stop=c == HC - 1 and n == 2,
                                       skip_group_check=True)
                if c == HC - 1:
                    mm.then_inc(y_ready, 1)

            def tile(s, u, w, load, nxt):
                nonlocal is_shared_now
                for c in range(HC):
                    if c < HC - 1:
                        up(s, u, w, c + 1)
                    elif nxt:
                        up(s + 1, nxt[0], nxt[1], 0, nxt[2])
                    down(s, u, w, c, load)
                    if c == 3 and nxt:
                        is_shared_now = nxt[3]
                        turn(s + 1, nxt[0])

            is_shared_now = True
            turn(0, 0)
            up(0, 0, 1, 0, 0)
            for s in range(HEAD):
                tile(s, s % 2, 1, 0, ((s + 1) % 2, 1, 0, True) if s < HEAD - 1 else (0, 0, 1, False))
            with pe.Fori(0, (TILES - 1) // 2) as i:
                for u in range(2):
                    s, load = HEAD + 2 * i + u, 2 * i + u + 1
                    tile(s, u, u, load, (1 - u, 1 - u, load + 1, False))
            tile(LAST - 1, 0, 0, TILES, (1, 1, TILES + 1, True))
            for s in range(LAST, END):
                tile(s, s % 2, 1, TILES + 1, ((s + 1) % 2, 1, TILES + 1, True) if s < END - 1 else None)

        def split(eng, load, w, c, lo):
            if c < HALF:
                k, cols = c // 2, slice((c % 2) * 512, (c % 2) * 512 + 512)
                raw, hi, low = w1raw[:, k, cols], w1hi[:, w, k, cols], w1lo[:, w, k, cols]
            else:
                n = 2 * (c - HALF)
                raw, hi, low = w2raw[:, n:n + 2, :], w2hi[:, w, n:n + 2, :], w2lo[:, w, n:n + 2, :]
            if lo:
                eng.wait_ge(w_hi, HC * load + c + 1)
                eng.tensor_tensor(low, raw, hi.bitcast(F32), ALU.subtract).then_inc(w_lo, 1)
            else:
                if c == 0:
                    eng.wait_ge(w1_in, 16 * (load + 1))
                if c == HALF:
                    eng.wait_ge(w2_in, 16 * (load + 1))
                eng.activation(hi, raw, ACT.Copy).then_inc(w_hi, 1)

        @block.scalar
        def _(act):
            for q in range(NT // C):
                act.wait_ge(gt_ready, 2 * q + 2)
                if q >= 2:
                    act.wait_ge(lg_ready, q - 1)
                act.activation(yT[:, q % 2, 0, :], ps[:, 2 * (q % 2), :], ACT.Copy).then_inc(gt_done, 1)
                act.activation(yT[:, q % 2, 1, :], ps[:, 2 * (q % 2) + 1, :], ACT.Copy).then_inc(gt_done, 1)
            act.wait_ge(gap_done, 1)
            act.activation(gap[:, :], gap[:, :], ACT.Exp).then_inc(gap_exp, 1)
            for c in range(HC):
                split(act, 0, 1, c, False)

            def turned(s, u):
                for k in range(DC):
                    act.wait_ge(tr_ready, 2 * s + k + 1)
                    act.activation(xhi[:, u, k, :], ps[:, 6 + k, :], ACT.Copy).then_inc(xhi_done, 1)

            def tile(s, u, w, nxt=None, load=None):
                for c in range(HC):
                    act.wait_ge(m1_ready, HC * s + c + 1)
                    if c == 0:
                        act.wait_ge(b_in, 32 * bias_loads)
                    act.activation(h[:, c % 2, :], ps[:, c % 2, :], ACT.Gelu, bias=bias1[:, w, c:c + 1]).then_inc(gelu_done, 1)
                    if c == 4 and nxt:
                        turned(s + 1, 1 - u)
                    if load is not None:
                        if c == 0:
                            act.wait_ge(y_ready, s)
                        split(act, load[0], load[1], c, False)

            turned(0, 0)
            for s in range(HEAD):
                bias_loads = 1
                tile(s, s % 2, 1, True, (1, 0) if s == HEAD - 1 else None)
            with act.Fori(0, (TILES - 1) // 2) as i:
                for u in range(2):
                    bias_loads = 2 * i + u + 2
                    tile(HEAD + 2 * i + u, u, u, True, (2 * i + u + 2, 1 - u))
            bias_loads = TILES + 1
            tile(LAST - 1, 0, 0, True, (TILES + 1, 1))
            bias_loads = TILES + 2
            for s in range(LAST, END):
                tile(s, s % 2, 1, s < END - 1)

        @block.gpsimd
        def _(pool):
            pool.memset(minus_half[:, :], -0.5).then_inc(minus_set, 1)
            pool.wait_ge(minus_set, 1)
            pool.wait_ge(slots_known, 1)
            for t in range(NT):
                for n in range(TOP):
                    pool.indirect_dma_start(slots_in, bass.IndirectOffsetOnAxis(ap=slot[:, n, t:t + 1], axis=0),
                                            res[:, t, :], None).then_inc(sent, 16)
                if t % C == C - 1:
                    pool.wait_ge(sent, 16 * TOP * (t + 1))

            def fetch(t):
                if t >= 4:
                    pool.wait_ge(c_step, 4 * (t - 4) + 2)
                for n in range(TOP):
                    pool.indirect_dma_start(back[:, t % 4, n, :], None, slots_out,
                                            bass.IndirectOffsetOnAxis(ap=slot[:, n, t:t + 1], axis=0)).then_inc(back_in[t % 4], 16)

            def root(t):
                pool.wait_ge(var_done, t + 1)
                pool.tensor_tensor(rstd[:, t % 2:t % 2 + 1], var[:, t % 2:t % 2 + 1], minus_half[:, :], ALU.pow).then_inc(rstd_done, 1)

            pool.wait_ge(y_out, 16 * TILES + 32)
            for t in range(NT + 4):
                if t < NT:
                    fetch(t)
                if t >= 4:
                    root(t - 4)

        @block.vector
        def _(dve):
            steps = 0

            def step(ins):
                nonlocal steps
                ins.then_inc(route_step, 1)
                steps += 1
                dve.wait_ge(route_step, steps)

            def over(ap, n):
                return ap.unsqueeze(2).to_broadcast([P, ap.shape[1], n])

            def across(ap, n):
                return ap.unsqueeze(1).to_broadcast([P, n, ap.shape[1]])

            dve.wait_ge(consts_in, 16 * CONSTS)
            for q in range(NT // C):
                dve.wait_ge(lg_ready, q + 1)
                dve.tensor_tensor(logits[:, C * q:C * (q + 1), :],
                                  ps[:, 4 + q % 2, 0:C * E].rearrange("p (c e) -> p c e", c=C),
                                  across(gb[:, :], C), ALU.add).then_inc(lg_done, 1)
            dve.wait_ge(lg_done, NT // C)
            rev = across(nums[:, 0:E], NT)

            def choose(values, top, into):
                step(dve.tensor_reduce(top[:, :], values[:, :, :], AX_X, ALU.max))
                step(dve.tensor_tensor(work[:, :, :], values[:, :, :], over(top[:, :], E), ALU.is_equal))
                step(dve.tensor_tensor(work[:, :, :], work[:, :, :], rev, ALU.mult))
                step(dve.tensor_reduce(pick[:, :], work[:, :, :], AX_X, ALU.max))
                step(dve.tensor_tensor(into[:, :, :], work[:, :, :], over(pick[:, :], E), ALU.is_equal))

            choose(logits, best, first)
            step(dve.scalar_tensor_tensor(both[:, :, :], first[:, :, :], -3.0e38, logits[:, :, :], ALU.mult, ALU.add))
            choose(both, next_best, second)
            step(dve.tensor_tensor(gap[:, :], next_best[:, :], best[:, :], ALU.subtract))
            dve.tensor_tensor(both[:, :, :], first[:, :, :], second[:, :, :], ALU.add).then_inc(both_done, 1)
            dve.sem_inc(gap_done, 1)
            dve.wait_ge(gap_exp, 1)
            step(dve.tensor_scalar(den[:, :], gap[:, :], 1.0, None, ALU.add))
            step(dve.reciprocal(wt[:, 0, :], den[:, :]))
            step(dve.tensor_tensor(wt[:, 1, :], gap[:, :], wt[:, 0, :], ALU.mult))
            step(dve.memset(zero[:, :], 0.0))
            dve.wait_ge(ranks_ready, 1)
            step(dve.tensor_copy(total[:, :, :], ps[:, 1, 0:NT * E].rearrange("p (t e) -> p e t", e=E)))
            step(dve.tensor_tensor_scan(upto[:, :, :].rearrange("p e t -> p (e t)"), total[:, :, :].rearrange("p e t -> p (e t)"),
                                        zero[:, :], 0.0, ALU.add, ALU.add))
            step(dve.tensor_tensor(total[:, :, :], upto[:, :, :], total[:, :, :], ALU.subtract))
            step(dve.tensor_tensor(count[:, :], upto[:, :, NT - 1], total[:, :, 0], ALU.subtract))
            step(dve.tensor_scalar(tiles_i[:, :], count[:, :], float(TS - 1), None, ALU.add))
            step(dve.tensor_scalar(tiles_i[:, :], tiles_i[:, :], TS.bit_length() - 1, None, ALU.arith_shift_right))
            step(dve.tensor_copy(tiles_f[:, :], tiles_i[:, :]))
            step(dve.tensor_tensor_scan(tiles_upto[:, :], tiles_f[:, :], zero[:, 0:E], 0.0, ALU.add, ALU.add))
            step(dve.tensor_tensor(base[:, :], tiles_upto[:, :], tiles_f[:, :], ALU.subtract))
            step(dve.scalar_tensor_tensor(base[:, :], base[:, :], float(TS), total[:, :, 0], ALU.mult, ALU.subtract))
            step(dve.tensor_tensor(total[:, :, :], total[:, :, :], over(base[:, :], NT), ALU.add))
            step(dve.tensor_tensor(work[:, :, :], ps[:, 0, 0:NT * E].rearrange("p (t e) -> p t e", e=E),
                                   total[:, :, :].rearrange("p e t -> p t e"), ALU.add))
            for n, hot in enumerate((first, second)):
                step(dve.tensor_tensor(hot[:, :, :], hot[:, :, :], work[:, :, :], ALU.mult))
                step(dve.tensor_reduce(slotf[:, n, :], hot[:, :, :], AX_X, ALU.add))
            step(dve.tensor_copy(slot[:, :, :], slotf[:, :, :]))
            step(dve.tensor_tensor(passed[:, :, :], across(tiles_upto[:, :], TILES), over(nums[:, E:], E), ALU.is_le))
            step(dve.tensor_reduce(owner[:, :], passed[:, :, :], AX_X, ALU.add))
            dve.tensor_scalar(owner_i[:, :], owner[:, :], float(E - 1), None, ALU.min).then_inc(slots_known, 1)

            for c in range(HC):
                split(dve, 0, 1, c, True)

            def turned(s, u):
                for k in range(DC):
                    dve.wait_ge(xhi_done, 2 * s + k + 1)
                    dve.tensor_tensor(xlo[:, u, k, :], ps[:, 6 + k, :], xhi[:, u, k, :].bitcast(F32), ALU.subtract).then_inc(xlo_done, 1)

            def halve(s, c):
                dve.wait_ge(gelu_done, HC * s + c + 1)
                dve.tensor_copy(hhi[:, c % 2, :], h[:, c % 2, :]).then_inc(hhi_done, 1)
                dve.wait_ge(hhi_done, HC * s + c + 1)
                dve.tensor_tensor(hlo[:, c % 2, :], h[:, c % 2, :], hhi[:, c % 2, :].bitcast(F32), ALU.subtract).then_inc(h_done, 1)

            def collect(s, u, w):
                dve.wait_ge(y_ready, s + 1)
                if is_shared_now:
                    if s < HEAD:
                        dve.wait_ge(sent, 16 * TOP * C * (s + 1))
                else:
                    dve.wait_ge(y_out, 16 * (s - HEAD) + 16)
                for a in range(2):
                    ins = dve.tensor_tensor(ys[:, u, 2 * a:2 * a + 2, :],
                                            ps[:, 2 + 2 * u + a, :].rearrange("p (c d) -> p c d", c=2),
                                            bias2[:, w, :].unsqueeze(1).to_broadcast([P, 2, D]), ALU.add)
                if not is_shared_now:
                    ins.then_inc(y_done, 1)
                else:
                    t = tokens(s)
                    n = s if s < HEAD else s - TILES
                    ins.then_inc(ysum, 1)
                    dve.wait_ge(ysum, n + 1)
                    dve.tensor_tensor(res[:, t[0]:t[-1] + 1, :], res[:, t[0]:t[-1] + 1, :], ys[:, u, :, :], ALU.add).then_inc(y_done, 1)

            done = 0

            def mix(t):
                nonlocal done
                g = t % 4
                shared = t // C if t // C < HEAD else t // C + TILES
                dve.wait_ge(y_done, shared + 1)
                dve.wait_ge(back_in[g], 32 * (t // 4 + 1))
                for n in range(TOP):
                    dve.scalar_tensor_tensor(res[:, t, :], back[:, g, n, :], wt[:, n, t:t + 1], res[:, t, :],
                                             ALU.mult, ALU.add).then_inc(c_step, 1)
                    done += 1
                    dve.wait_ge(c_step, done)
                dve.bn_stats(bn[:, t % 2, :], res[:, t, :]).then_inc(c_step, 1)
                dve.wait_ge(c_step, done + 1)
                dve.bn_aggr(mv[:, t % 2, :], bn[:, t % 2, :]).then_inc(c_step, 1)
                done += 2
                dve.wait_ge(c_step, done)
                dve.tensor_scalar(var[:, t % 2:t % 2 + 1], mv[:, t % 2, 1:2], EPS, None, ALU.add).then_inc(var_done, 1)

            def finish(t):
                dve.wait_ge(rstd_done, t + 1)
                if t >= 4:
                    dve.wait_ge(fin_out[t % 4], 16 * (t // 4))
                dve.tensor_scalar(fin[:, t % 4, :], res[:, t, :], mv[:, t % 2, 0:1], rstd[:, t % 2:t % 2 + 1],
                                  ALU.subtract, ALU.mult).then_inc(fin_done, 1)

            def combine(n):
                if 0 <= n < NT:
                    mix(n)
                if 0 <= n - 1 < NT:
                    finish(n - 1)

            def tile(s, u, w, nxt=True, load=None, at=None):
                for c in range(HC):
                    if c < HC - 1:
                        halve(s, c + 1)
                    elif nxt:
                        halve(s + 1, 0)
                    if load is not None:
                        split(dve, load[0], load[1], c, True)
                    if c == 4 and nxt:
                        turned(s + 1, 1 - u)
                    if at is not None:
                        combine(at + c - LAG)
                collect(s, u, w)

            turned(0, 0)
            halve(0, 0)
            is_shared_now = True
            for s in range(HEAD):
                tile(s, s % 2, 1, True, (1, 0) if s == HEAD - 1 else None)
            is_shared_now = False
            with dve.Fori(0, (TILES - 1) // 2) as i:
                for u in range(2):
                    tile(HEAD + 2 * i + u, u, u, True, (2 * i + u + 2, 1 - u))
            tile(LAST - 1, 0, 0, True, (TILES + 1, 1))
            is_shared_now = True
            for s in range(LAST, END):
                tile(s, s % 2, 1, s < END - 1, None, HC * (s - LAST))
            for n in range(HC * LASTS - LAG, NT + 1):
                combine(n)


def host_constants():
    inv = np.float32(10000.0) ** (-np.arange(0, DR, 2, dtype=np.float32) / np.float32(DR))
    ang = np.arange(S, dtype=np.float32)[:, None] * inv
    rope = np.zeros((P, 2, S), np.float32)
    rope[:, 0, :] = 1.0
    for i in range(HG):
        for r in range(DR):
            row = SLOT * i + DH + r
            rope[row, 0] = np.cos(ang[:, r // 2])
            rope[row, 1] = np.sin(ang[:, r // 2]) * (-1.0 if r % 2 == 0 else 1.0)
    masks = np.zeros((P, 5, P), np.float32)
    for m in range(P):
        masks[SLOT * (m // SLOT) + DH, 0, m] = 1.0
    masks[:, 1, :] = np.eye(P)
    masks[:, 2, :] = np.triu(np.ones((P, P)), 1)
    masks[:, 3, :] = 1.0
    masks[:, 4, :] = np.triu(np.ones((P, P)))
    numbers = np.zeros((P, E + TILES), np.float32)
    numbers[:, :E] = E - np.arange(E)
    numbers[:, E:] = np.arange(TILES)
    return rope, masks, numbers


def attention_layouts(x, W_DQ, W_UQ, W_QR, W_DKV, W_UK, W_UV, W_KR, W_O):
    xf = x.reshape(T, D)
    x_tok = np.ascontiguousarray(xf.reshape(NT, P, D).transpose(1, 0, 2))
    x_t = np.ascontiguousarray(xf.T.reshape(DC, P, T).transpose(1, 0, 2))
    w_down = np.concatenate([W_DQ, W_DKV], axis=1).reshape(DC, P, 2 * LAT).transpose(1, 0, 2)
    partner = np.arange(DR) ^ 1
    w_q = np.zeros((LAT, 2, H, SLOT), np.float32)
    w_q[:, 0, :, :DH] = W_UQ.reshape(LAT, H, DH)
    w_q[:, 0, :, DH:DH + DR] = W_QR.reshape(LAT, H, DR)
    w_q[:, 1, :, DH:DH + DR] = W_QR.reshape(LAT, H, DR)[:, :, partner]
    w_q = w_q.reshape(LAT, 2, G, P).transpose(0, 2, 1, 3)
    w_k = np.zeros((LAT, H, SLOT), np.float32)
    w_k[:, :, :DH] = W_UK.reshape(LAT, H, DH)
    w_kv = np.concatenate([w_k.reshape(LAT, G * P), W_UV], axis=1)
    w_kr = np.zeros((D, 2, HG, SLOT), np.float32)
    w_kr[:, 0, :, DH:DH + DR] = W_KR[:, None, :]
    w_kr[:, 1, :, DH:DH + DR] = W_KR[:, None, partner]
    w_kr = w_kr.reshape(DC, P, 2, P).transpose(1, 0, 2, 3)
    w_o = np.zeros((G, HG, SLOT, D), np.float32)
    w_o[:, :, :DH] = W_O.reshape(G, HG, DH, D)
    w_o = w_o.reshape(G, P, D).transpose(1, 0, 2)
    return [np.ascontiguousarray(a) for a in (x_tok, x_t, w_down, w_q, w_kv, w_kr, w_o)]


def build(nc, x, xT, w_down, w_q, w_kv, w_kr, w_o, w1, w2, b1, b2, gate_w, gate_b, rope, masks, numbers, out):
    slots_in = nc.dram_tensor("slots_in", (SLOTS, D), F32, kind="Internal").ap()
    slots_out = nc.dram_tensor("slots_out", (SLOTS, D), F32, kind="Internal").ap()
    with nc.sbuf_tensor("res", [P, NT, D], F32) as res:
        attention(nc, x, xT, w_down, w_q, w_kv, w_kr, w_o, rope, masks, res, slots_in)
        experts(nc, res, slots_in, slots_out, w1, w2, b1, b2, gate_w, gate_b, masks, numbers, out)


_INS = ["x", "xT", "w_down", "w_q", "w_kv", "w_kr", "w_o", "w1", "w2", "b1", "b2", "gate_w", "gate_b",
        "rope", "masks", "numbers"]


def kernel(L0_attn_x, L0_attn_W_DQ, L0_attn_W_UQ, L0_attn_W_QR, L0_attn_W_DKV, L0_attn_W_UK, L0_attn_W_UV,
           L0_attn_W_KR, L0_attn_W_O, L0_ffn_gate_w, L0_ffn_gate_b, L0_ffn_w1, L0_ffn_b1, L0_ffn_w2, L0_ffn_b2,
           L0_ffn_ws1, L0_ffn_bs1, L0_ffn_ws2, L0_ffn_bs2):
    import concourse.bacc as bacc
    from concourse.bass_utils import run_bass_kernel_spmd

    a = lambda v: np.asarray(v)
    laid = attention_layouts(a(L0_attn_x), a(L0_attn_W_DQ), a(L0_attn_W_UQ), a(L0_attn_W_QR), a(L0_attn_W_DKV),
                             a(L0_attn_W_UK), a(L0_attn_W_UV), a(L0_attn_W_KR), a(L0_attn_W_O))
    w1 = np.concatenate([a(L0_ffn_w1), a(L0_ffn_ws1)[None]])
    w2 = np.concatenate([a(L0_ffn_w2), a(L0_ffn_ws2)[None]])
    b1 = np.concatenate([a(L0_ffn_b1), a(L0_ffn_bs1)[None]]).reshape(E + 1, HID // P, P).transpose(0, 2, 1)
    b2 = np.concatenate([a(L0_ffn_b2), a(L0_ffn_bs2)[None]])
    arrays = dict(zip(_INS, laid + [w1, w2, b1, b2, a(L0_ffn_gate_w), a(L0_ffn_gate_b), *host_constants()]))
    arrays = {n: np.ascontiguousarray(v) for n, v in arrays.items()}
    nc = bacc.Bacc("TRN2", target_bir_lowering=False, num_devices=1)
    aps = [nc.dram_tensor(n, v.shape, mybir.dt.from_np(v.dtype), kind="ExternalInput").ap() for n, v in arrays.items()]
    out = nc.dram_tensor("out", (T, D), F32, kind="ExternalOutput").ap()
    build(nc, *aps, out)
    r = run_bass_kernel_spmd(nc, [arrays], core_ids=[0])
    return r.results[0]["out"].reshape(B, S, D)
```

```python
from contextlib import ExitStack

import numpy as np
import concourse.bass as bass
from concourse import mybir

F32 = mybir.dt.float32
F32R = mybir.dt.float32r
I32 = mybir.dt.int32
ALU = mybir.AluOpType
ACT = mybir.ActivationFunctionType
AX_X = mybir.AxisListType.X

P = 128
B, S, D = 8, 512, 256
T = B * S
NT = T // P
H, DH, DR = 16, 16, 8
LAT = 64
SLOT = 32
HG = P // SLOT
G = H // HG
KB = S // P
DC = D // P
SCALE = 1.0 / float(np.sqrt(np.float32(DH + DR)))
E, HID = 8, 1024
TOP = 2
TS = 512
TILES = TOP * T // TS + E - 1
SLOTS = TILES * TS
CLIP = 80.0
EPS = 1e-5

COLS = [S - P * j for j in range(KB)]
AT = [0, S, 2 * S, S + COLS[1]]
EW = sum(COLS)
SCORE_AT = [0, S, 3 * S - COLS[2], 2 * S]
SCORE_FROM = [0, P, 2 * P, 2 * P]
PARTS = 3
AHEAD = 2


def attention(nc, x, xT, w_down, w_q, w_kv, w_kr, w_o, rope, masks, res, slots_in):
    QK_AT = {4: 0, 5: 1, 10: 2, 11: 3}
    C_AT, V_AT, FLIP_AT, O_AT = 1, 2, 3, 6
    V_COPY_AT = {0: 3, 6: 0, 9: 1, 13: 2}

    with ExitStack() as ctx:
        def sb(name, shape, dt=F32):
            return ctx.enter_context(nc.sbuf_tensor(name, shape, dt))

        def sem(name):
            return ctx.enter_context(nc.semaphore(name))

        xt = sb("xt", [P, DC, S])
        wd = sb("wd", [P, DC, 2 * LAT])
        wq = sb("wq", [LAT, G, 2, P])
        wkv = sb("wkv", [P, G * P + D])
        wkr = sb("wkr", [P, DC, 2, P])
        wo = sb("wo", [P, DC, D])
        cs = sb("cs", [P, 2, S])
        pick, ident = sb("slot_pick", [P, P]), sb("ident1", [P, P])
        cT = sb("cT", [P, S])
        kr, krsin = sb("kr", [P, S]), sb("krsin", [P, S])
        sinpart = sb("sinpart", [P, 2, S])
        qt, kt = sb("qt", [P, 2, S]), sb("kt", [P, 2, S])
        qhi, qlo, khi, klo = (sb(n, [P, 2, S], F32R) for n in ("qhi", "qlo", "khi", "klo"))
        qs, ks = sb("qs", [PARTS * SLOT, H, S], F32R), sb("ks", [PARTS * SLOT, H, S], F32R)
        v = sb("v", [P, KB, H, SLOT])
        vnext = sb("vnext", [P, KB, H, DH])
        e = sb("e", [P, 4, EW])
        ot = sb("ot", [P, 2, S])
        rec = sb("rec", [P, 2, KB, HG])
        onq = sb("onq", [P, KB, H * DH])
        on = sb("on", [P, DC, S])
        bn = sb("bn", [P, KB, 6])
        mv = sb("mv", [P, KB, 2])
        var = sb("var", [P, KB])
        rstd = sb("rstd", [P, KB])
        minus_half = sb("minus_half", [P, KB])
        row = sb("row", [P, KB, D])
        causal = sb("causal", [P, 2, P])
        zeros = sb("zeros", [P, 1, D])
        ps = ctx.enter_context(nc.psum_tensor("ps", [P, 8, S], F32))
        SC, PROJ, PV = 0, 3, 6

        consts_in = sem("consts_in")
        xt_in, rows_in = sem("xt_in"), sem("rows_in")
        ones_set = sem("ones_set")
        c_ready, ct_done = sem("c_ready"), sem("ct_done")
        kr_ready, kr_steps = sem("kr_ready"), sem("kr_steps")
        v_ready, v_done, v_placed = sem("v_ready"), sem("v_done"), sem("v_placed")
        qk_ready, rope_steps, q_done = sem("qk_ready"), sem("rope_steps"), sem("q_done")
        hi_done, lo_done, stacked = sem("hi_done"), sem("lo_done"), sem("stacked")
        s01_ready, exp01_done = sem("s01_ready"), sem("exp01_done")
        s_ready, exp_done, clip_done, mask_done = sem("s_ready"), sem("exp_done"), sem("clip_done"), sem("mask_done")
        pv_done, ot_done, turned, rec_done, normed = sem("pv_done"), sem("ot_done"), sem("turned"), sem("rec_done"), sem("normed")
        flipped, on_done = sem("flipped"), sem("on_done")
        a_ready, res_done, bn_done, mv_done = sem("a_ready"), sem("res_done"), sem("bn_done"), sem("mv_done")
        var_done, rstd_done = sem("var_done"), sem("rstd_done")
        zeros_set, slots_zeroed = sem("zeros_set"), sem("slots_zeroed")

        block = ctx.enter_context(nc.Block())
        CONSTS = 10
        PICKED = HG * (DH + 1)
        STACK = 16 * HG * 2 * PARTS

        @block.sync
        def _(sp):
            def load_xt(b):
                sp.dma_start(xt[:, :, :], xT[:, :, bass.ds(b * S, S)]).then_inc(xt_in, 16)

            def stack(b, pair, first=False):
                last = G * b + 2 * pair + 1
                if not first:
                    sp.wait_ge(s_ready, H * (b - 1) + 2 * HG * (pair + 1))
                for part, src, dst, rows in ((1, khi, ks, (0, 1)), (2, qhi, qs, (0, 2)),
                                             (1, klo, ks, (2,)), (2, qlo, qs, (1,))):
                    sp.wait_ge(hi_done if src in (khi, qhi) else lo_done, 2 * last + part)
                    for i in range(HG):
                        heads = slice(2 * HG * pair + i, 2 * HG * pair + HG + i + 1, HG)
                        for r in rows:
                            sp.dma_start(dst[SLOT * r:SLOT * (r + 1), heads, :].bitcast(F32),
                                         src[SLOT * i:SLOT * (i + 1), :, :].bitcast(F32)).then_inc(stacked, 16)

            def batch(b, load):
                if load:
                    sp.wait_ge(kr_ready, b + 2)
                    load_xt(b + 2)
                for pair in range(2):
                    stack(b + 1, pair)

            sp.dma_start(xt[:, :, :], xT[:, :, 0:S]).then_inc(xt_in, 16)
            for dst, src in ((wd, w_down), (wkr, w_kr), (cs, rope)):
                sp.dma_start(dst[:], src).then_inc(consts_in, 16)
            sp.dma_start(wkv[LAT:P, :], w_kv).then_inc(consts_in, 16)
            sp.dma_start(wq[:], w_q).then_inc(consts_in, 16)
            for n in range(2):
                sp.dma_start(causal[:, n, :], masks[:, 4, :]).then_inc(consts_in, 16)
            sp.dma_start(pick[:], masks[:, 0, :]).then_inc(consts_in, 16)
            sp.dma_start(ident[:], masks[:, 1, :]).then_inc(consts_in, 16)
            sp.dma_start(wo[:], w_o).then_inc(consts_in, 16)
            sp.wait_ge(kr_ready, 1)
            load_xt(1)
            for pair in range(2):
                stack(0, pair, first=True)
            for b in range(B):
                sp.dma_start(res[:, b * KB:(b + 1) * KB, :], x[:, b * KB:(b + 1) * KB, :]).then_inc(rows_in, 16)
            with sp.Fori(0, B - 2) as b:
                batch(b, True)
            batch(B - 2, False)
            sp.wait_ge(zeros_set, 1)
            with sp.Fori(0, TILES) as n:
                sp.dma_start(slots_in[bass.ds(n * TS, TS), :].rearrange("(p c) d -> p c d", p=P),
                             zeros[:, :, :].to_broadcast([P, TS // P, D])).then_inc(slots_zeroed, 16)
            sp.wait_ge(slots_zeroed, 16 * TILES)
            sp.wait_ge(xt_in, 16 * B)
            sp.wait_ge(rows_in, 16 * B)

        @block.tensor
        def _(pe):
            def latents(b):
                pe.wait_ge(xt_in, 16 * (b + 1))
                for k in range(DC):
                    mm = pe.matmul(ps[:, PROJ, :], wd[:, k, :], xt[:, k, :], start=k == 0, stop=k == DC - 1)
                mm.then_inc(c_ready, 1)

            def rotary_keys(b):
                for r in range(2):
                    for k in range(DC):
                        mm = pe.matmul(ps[:, PROJ + 1 + r, :], wkr[:, k, r, :], xt[:, k, :],
                                       start=k == 0, stop=k == DC - 1)
                mm.then_inc(kr_ready, 1)

            def values(b):
                pe.wait_ge(kr_steps, 3 * b + 2)
                pe.wait_ge(ct_done, b + 1)
                for t in range(KB):
                    mm = pe.matmul(ps[:, PROJ + 1 + t // 2, (t % 2) * D:(t % 2) * D + D], cT[LAT:P, t * P:(t + 1) * P],
                                   wkv[LAT:P, G * P:], start=True, stop=True)
                    if t % 2:
                        mm.then_inc(v_ready, 1)

            def queries_keys(b, g, first=False):
                if g == 0:
                    pe.wait_ge(v_done, 2 * b + 2)
                    if not first:
                        pe.wait_ge(on_done, DC * (b - 1))
                else:
                    pe.wait_ge(rope_steps, 3 * (G * b + g))
                pe.matmul(ps[:, PROJ + 2, :], wkv[LAT:P, g * P:(g + 1) * P], cT[LAT:P, :], start=True, stop=True)
                pe.matmul(ps[:, PROJ, :], wq[:, g, 0, :], cT[0:LAT, :], start=True, stop=True)
                pe.matmul(ps[:, PROJ + 1, :], wq[:, g, 1, :], cT[0:LAT, :],
                          start=True, stop=True).then_inc(qk_ready, 1)

            def scores(b, h, first=False):
                if h % (2 * HG) == 0:
                    pe.wait_ge(stacked, STACK * (2 * b + h // (2 * HG) + 1))
                for j in range(KB):
                    if j % 2 == 0 and not first:
                        pe.wait_ge(exp_done if j else exp01_done, H * b + h)
                    bank, col = SC + SCORE_AT[j] // S, SCORE_AT[j] % S
                    mm = pe.matmul(ps[:, bank, col:col + S - SCORE_FROM[j]], ks[:, h, P * j:P * (j + 1)],
                                   qs[:, h, SCORE_FROM[j]:], start=True, stop=True)
                    if j % 2:
                        mm.then_inc(s_ready if j == 3 else s01_ready, 1)

            def weigh(b, h, first=False):
                g, i = h // HG, h % HG
                if i == 0:
                    pe.wait_ge(v_placed, G * b + g + 1)
                    if not (first and g < 2):
                        pe.wait_ge(normed, G * b + g - 1)
                pe.wait_ge(mask_done, H * b + h + 1)
                for j in range(KB):
                    mm = pe.matmul(ps[SLOT * i:SLOT * (i + 1), PV + g % 2, P * j:], v[:, j, h, :],
                                   e[:, h % 4, AT[j]:AT[j] + COLS[j]], start=j == 0, stop=j == KB - 1)
                mm.then_inc(pv_done, 1)

            def turn(b, g):
                pe.wait_ge(ot_done, G * b + g + 1)
                for t in range(KB):
                    mm = pe.matmul(ps[:, PV + g % 2, t * PICKED:(t + 1) * PICKED], ot[:, g % 2, t * P:(t + 1) * P],
                                   pick[:, 0:PICKED], start=True, stop=True)
                mm.then_inc(turned, 1)

            def flip(b):
                pe.wait_ge(normed, G * (b + 1))
                for c in range(DC):
                    for t in range(KB):
                        mm = pe.matmul(ps[:, PROJ + c, t * P:(t + 1) * P], onq[:, t, c * P:(c + 1) * P], ident[:, :],
                                       start=True, stop=True)
                    mm.then_inc(flipped, 1)

            def output(b):
                pe.wait_ge(on_done, DC * (b + 1))
                for t in range(KB):
                    for c in range(DC):
                        mm = pe.matmul(ps[:, PROJ + t // 2, (t % 2) * D:(t % 2) * D + D], on[:, c, t * P:(t + 1) * P],
                                       wo[:, c, :], start=c == 0, stop=c == DC - 1)
                    if t % 2:
                        mm.then_inc(a_ready, 1)

            def batch(b, first=False, last=False):
                for h in range(H):
                    if h + AHEAD < H:
                        scores(b, h + AHEAD)
                    elif not last:
                        scores(b + 1, h + AHEAD - H)
                    if h == C_AT and not last:
                        pe.wait_ge(rope_steps, 3 * G * (b + 1))
                        latents(b + 1)
                        rotary_keys(b + 1)
                    if h == V_AT and not last:
                        values(b + 1)
                    if h == FLIP_AT and not first:
                        if last:
                            pe.wait_ge(rope_steps, 3 * G * (b + 1))
                        else:
                            pe.wait_ge(v_done, 2 * b + 3)
                        flip(b - 1)
                    if h in QK_AT and not last:
                        if QK_AT[h] == 2 and not first:
                            pe.wait_ge(res_done, KB * b)
                        queries_keys(b + 1, QK_AT[h], first)
                    if h == O_AT and not first:
                        if not last:
                            pe.wait_ge(rope_steps, 3 * (G * (b + 1) + 2))
                        output(b - 1)
                    weigh(b, h, first)
                    if h % HG == 0 and h:
                        turn(b, h // HG - 1)
                    elif h == 0 and not first:
                        turn(b - 1, G - 1)

            pe.wait_ge(consts_in, 16 * CONSTS)
            pe.wait_ge(ones_set, 1)
            latents(0)
            rotary_keys(0)
            values(0)
            for g in range(2):
                queries_keys(0, g, first=True)
            for h in range(AHEAD):
                scores(0, h, first=h == 0)
            for g in range(2, G):
                queries_keys(0, g)
            batch(0, first=True)
            with pe.Fori(1, B - 1) as b:
                batch(b)
            batch(B - 1, last=True)
            turn(B - 1, G - 1)
            flip(B - 1)
            output(B - 1)

        @block.scalar
        def _(act):
            def latents(b):
                act.wait_ge(c_ready, b + 1)
                act.activation(cT[:, :], ps[:, PROJ, :], ACT.Copy).then_inc(ct_done, 1)

            def values(b, first=False):
                for n in range(2):
                    if n == 0 and not first:
                        act.wait_ge(v_placed, G * b)
                    act.wait_ge(v_ready, 2 * b + n + 1)
                    act.activation(vnext[:, 2 * n:2 * n + 2, :, :],
                                   ps[:, PROJ + 1 + n, :].rearrange("p (t h d) -> p t h d", t=2, h=H),
                                   ACT.Copy).then_inc(v_done, 1)

            def place_values(b, g, first=False):
                if not first:
                    act.wait_ge(pv_done, H * (b - 1) + HG * (g + 1))
                act.wait_ge(v_done, 2 * b + 2)
                act.activation(v[:, :, HG * g:HG * (g + 1), 0:DH],
                               vnext[:, :, HG * g:HG * (g + 1), :], ACT.Copy).then_inc(v_placed, 1)

            def high_parts(b, g, first=False):
                n = G * b + g
                if g % 2 == 0 and not first:
                    act.wait_ge(stacked, STACK * (2 * b + g // 2))
                act.wait_ge(rope_steps, 3 * n + 1)
                act.activation(khi[:, g % 2, :], kt[:, g % 2, :], ACT.Copy).then_inc(hi_done, 1)
                act.wait_ge(q_done, n + 1)
                act.activation(qhi[:, g % 2, :], qt[:, g % 2, :], ACT.Copy).then_inc(hi_done, 1)

            def exps(b, h, first=False):
                act.wait_ge(s01_ready, H * b + h + 1)
                if not (first and h < 4):
                    act.wait_ge(pv_done, H * b + h - 3)
                act.activation(e[:, h % 4, 0:AT[2] - P], ps[:, SC:SC + 2, :].rearrange("p a s -> p (a s)")[:, 0:AT[2] - P],
                               ACT.Exp, scale=SCALE).then_inc(exp01_done, 1)
                act.wait_ge(s_ready, H * b + h + 1)
                act.activation(e[:, h % 4, AT[2] - P:EW], ps[:, SC + 2, P:], ACT.Exp, scale=SCALE).then_inc(exp_done, 1)

            def outputs(b, g, first=False):
                act.wait_ge(pv_done, H * b + HG * (g + 1))
                if not (first and g < 2):
                    act.wait_ge(turned, G * b + g - 1)
                act.activation(ot[:, g % 2, :], ps[:, PV + g % 2, :], ACT.Copy).then_inc(ot_done, 1)

            def flips(b):
                for c in range(DC):
                    act.wait_ge(flipped, DC * b + c + 1)
                    act.activation(on[:, c, :], ps[:, PROJ + c, :], ACT.Copy).then_inc(on_done, 1)

            def batch(b, first=False, last=False):
                for h in range(H):
                    if h + AHEAD < H:
                        exps(b, h + AHEAD, first)
                    elif not last:
                        exps(b + 1, h + AHEAD - H)
                    if h % HG == 0 and h:
                        outputs(b, h // HG - 1, first)
                    elif h == 0 and not first:
                        outputs(b - 1, G - 1)
                    if h - 1 in QK_AT and not last:
                        high_parts(b + 1, QK_AT[h - 1])
                    if h == C_AT and not last:
                        latents(b + 1)
                    if V_COPY_AT.get(h) == 3:
                        place_values(b, 3, first)
                    elif h in V_COPY_AT and not last:
                        place_values(b + 1, V_COPY_AT[h])
                    if h == V_AT and not last:
                        values(b + 1)
                    if h == FLIP_AT and not first:
                        flips(b - 1)

            latents(0)
            values(0, first=True)
            for g in range(G - 1):
                place_values(0, g, first=True)
            for g in range(2):
                high_parts(0, g, first=True)
            for h in range(AHEAD):
                exps(0, h, first=True)
            for g in range(2, G):
                high_parts(0, g)
            batch(0, first=True)
            with act.Fori(1, B - 1) as b:
                batch(b)
            batch(B - 1, last=True)
            outputs(B - 1, G - 1)
            flips(B - 1)

        @block.gpsimd
        def _(pool):
            def rotate(b, g):
                n = G * b + g
                pool.wait_ge(rope_steps, 3 * n + 3)
                pool.tensor_tensor(qt[:, g % 2, :], qt[:, g % 2, :], sinpart[:, g % 2, :], ALU.add).then_inc(q_done, 1)

            def mask(b, h):
                pool.wait_ge(clip_done, H * b + h + 1)
                a = e[:, h % 4, 0:2 * S].rearrange("p (a s) -> p a s", a=2)[:, :, 0:P]
                c = e[:, h % 4, AT[3]:AT[2] + P].rearrange("p (a s) -> p a s", a=2)
                pool.tensor_tensor(a, a, causal[:, :, :], ALU.mult)
                pool.tensor_tensor(c, c, causal[:, :, :], ALU.mult).then_inc(mask_done, 1)

            def deviations(b):
                pool.wait_ge(var_done, b + 1)
                pool.tensor_tensor(rstd[:, :], var[:, :], minus_half[:, :], ALU.pow).then_inc(rstd_done, 1)

            def batch(b, first=False, last=False):
                for h in range(H):
                    if h + AHEAD < H:
                        mask(b, h + AHEAD)
                    elif not last:
                        mask(b + 1, h + AHEAD - H)
                    if h in QK_AT and not last:
                        rotate(b + 1, QK_AT[h])
                    if h == O_AT + 1 and not first:
                        deviations(b - 1)

            pool.memset(v[:, :, :, DH:], 1.0).then_inc(ones_set, 1)
            pool.memset(minus_half[:, :], -0.5)
            pool.memset(zeros[:, :, :], 0.0).then_inc(zeros_set, 1)
            pool.wait_ge(consts_in, 16 * CONSTS)
            for g in range(2):
                rotate(0, g)
            for h in range(AHEAD):
                mask(0, h)
            for g in range(2, G):
                rotate(0, g)
            batch(0, first=True)
            with pool.Fori(1, B - 1) as b:
                batch(b)
            batch(B - 1, last=True)
            deviations(B - 1)

        @block.vector
        def _(dve):
            low, high = float(np.exp(-CLIP * SCALE)), float(np.exp(CLIP * SCALE))

            def rotary_keys(b, first=False):
                if not first:
                    dve.wait_ge(rope_steps, 3 * G * b)
                dve.wait_ge(kr_ready, b + 1)
                dve.tensor_tensor(kr[:, :], ps[:, PROJ + 1, :], cs[:, 0, :], ALU.mult).then_inc(kr_steps, 1)
                dve.tensor_tensor(krsin[:, :], ps[:, PROJ + 2, :], cs[:, 1, :], ALU.mult).then_inc(kr_steps, 1)
                dve.wait_ge(kr_steps, 3 * b + 2)
                dve.tensor_tensor(kr[:, :], kr[:, :], krsin[:, :], ALU.add).then_inc(kr_steps, 1)

            def rotate(b, g, first=False):
                n = G * b + g
                if g == 0:
                    dve.wait_ge(kr_steps, 3 * b + 3)
                if not (first and g < 2):
                    dve.wait_ge(lo_done, 2 * n - 2)
                dve.wait_ge(qk_ready, n + 1)
                dve.tensor_tensor(kt[:, g % 2, :], ps[:, PROJ + 2, :], kr[:, :], ALU.add).then_inc(rope_steps, 1)
                dve.tensor_tensor(qt[:, g % 2, :], ps[:, PROJ, :], cs[:, 0, :], ALU.mult).then_inc(rope_steps, 1)
                dve.tensor_tensor(sinpart[:, g % 2, :], ps[:, PROJ + 1, :], cs[:, 1, :], ALU.mult).then_inc(rope_steps, 1)

            def low_parts(b, g, first=False):
                n = G * b + g
                if g % 2 == 0 and not first:
                    dve.wait_ge(stacked, STACK * (2 * b + g // 2))
                for part, lo, full, hi in ((1, klo, kt, khi), (2, qlo, qt, qhi)):
                    dve.wait_ge(hi_done, 2 * n + part)
                    dve.tensor_tensor(lo[:, g % 2, :], full[:, g % 2, :], hi[:, g % 2, :].bitcast(F32),
                                      ALU.subtract).then_inc(lo_done, 1)

            def clip(b, h):
                dve.wait_ge(exp_done, H * b + h + 1)
                dve.tensor_scalar(e[:, h % 4, :], e[:, h % 4, :], high, low, ALU.min, ALU.max).then_inc(clip_done, 1)

            def normalise(b, g, first=False):
                n = G * b + g
                if g == 0 and not first:
                    dve.wait_ge(flipped, DC * b)
                dve.wait_ge(turned, n + 1)
                both = ps[:, PV + g % 2, 0:KB * PICKED].rearrange("p (t w) -> p t w", t=KB)
                dve.reciprocal(rec[:, g % 2, :, :], both[:, :, HG * DH:]).then_inc(rec_done, 1)
                dve.wait_ge(rec_done, n + 1)
                dve.tensor_tensor(onq[:, :, g * HG * DH:(g + 1) * HG * DH].rearrange("p t (i d) -> p t i d", i=HG),
                                  both[:, :, 0:HG * DH].rearrange("p t (i d) -> p t i d", i=HG),
                                  rec[:, g % 2, :, :].unsqueeze(3).to_broadcast([P, KB, HG, DH]),
                                  ALU.mult).then_inc(normed, 1)

            def residual(b):
                for t in range(KB):
                    if t % 2 == 0:
                        dve.wait_ge(a_ready, 2 * b + t // 2 + 1)
                    dve.tensor_tensor(row[:, t, :], ps[:, PROJ + t // 2, (t % 2) * D:(t % 2) * D + D],
                                      res[:, bass.ds(b * KB + t, 1), :].rearrange("p a d -> p (a d)"),
                                      ALU.add).then_inc(res_done, 1)
                    dve.wait_ge(res_done, KB * b + t + 1)
                    dve.bn_stats(bn[:, t, :], row[:, t, :]).then_inc(bn_done, 1)

            def variance(b):
                dve.wait_ge(consts_in, 16 * CONSTS)
                dve.wait_ge(bn_done, KB * b + KB)
                for t in range(KB):
                    dve.bn_aggr(mv[:, t, :], bn[:, t, :]).then_inc(mv_done, 1)
                dve.wait_ge(mv_done, KB * (b + 1))
                dve.tensor_scalar(var[:, :], mv[:, :, 1], EPS, None, ALU.add).then_inc(var_done, 1)

            def layernorm(b):
                dve.wait_ge(rstd_done, b + 1)
                for t in range(KB):
                    dve.tensor_scalar(res[:, bass.ds(b * KB + t, 1), :].rearrange("p a d -> p (a d)"), row[:, t, :],
                                      mv[:, t, 0:1], rstd[:, t:t + 1], ALU.subtract, ALU.mult)

            def batch(b, first=False, last=False):
                for h in range(H):
                    if h + AHEAD < H:
                        clip(b, h + AHEAD)
                    elif not last:
                        clip(b + 1, h + AHEAD - H)
                    if h in QK_AT and not last:
                        rotate(b + 1, QK_AT[h])
                    if h % HG == 1 and h > HG:
                        normalise(b, h // HG - 1, first)
                    elif h == 1 and not first:
                        normalise(b - 1, G - 1)
                    if h - 2 in QK_AT and not last:
                        low_parts(b + 1, QK_AT[h - 2])
                    if h == O_AT and not first:
                        residual(b - 1)
                        variance(b - 1)
                    if h == C_AT and not last:
                        rotary_keys(b + 1)
                    if h == O_AT + 2 and not first:
                        layernorm(b - 1)

            dve.wait_ge(consts_in, 16 * CONSTS)
            rotary_keys(0, first=True)
            for g in range(2):
                rotate(0, g, first=True)
                low_parts(0, g, first=True)
            for h in range(AHEAD):
                clip(0, h)
            for g in range(2, G):
                rotate(0, g)
                low_parts(0, g)
            batch(0, first=True)
            dve.wait_ge(rows_in, 16 * B)
            with dve.Fori(1, B - 1) as b:
                batch(b)
            batch(B - 1, last=True)
            normalise(B - 1, G - 1)
            residual(B - 1)
            variance(B - 1)
            layernorm(B - 1)


def experts(nc, res, slots_in, slots_out, w1, w2, b1, b2, gate_w, gate_b, masks, numbers, out):
    C = TS // P
    HC = HID // P
    HEAD = 4
    LAST = HEAD + TILES
    END = T // TS + TILES
    PIECE = DC * HID // HC * 2
    HALF = HC // 2
    with ExitStack() as ctx:
        def sb(name, shape, dt=F32):
            return ctx.enter_context(nc.sbuf_tensor(name, shape, dt))

        def sem(name):
            return ctx.enter_context(nc.semaphore(name))

        w1raw, w2raw = sb("w1raw", [P, DC, HID]), sb("w2raw", [P, HC, D])
        w1hi, w1lo = sb("w1hi", [P, 2, DC, HID], F32R), sb("w1lo", [P, 2, DC, HID], F32R)
        w2hi, w2lo = sb("w2hi", [P, 2, HC, D], F32R), sb("w2lo", [P, 2, HC, D], F32R)
        bias1, bias2 = sb("bias1", [P, 2, HC]), sb("bias2", [P, 2, D])
        rows = sb("rows", [P, 2, C, D])
        xhi, xlo = sb("xhi", [P, 2, DC, TS], F32R), sb("xlo", [P, 2, DC, TS], F32R)
        yT = sb("yT", [P, 2, DC, TS])
        h = sb("h", [P, 2, TS])
        hhi, hlo = sb("hhi", [P, 2, TS], F32R), sb("hlo", [P, 2, TS], F32R)
        ys = sb("ys", [P, 2, C, D])
        ident, before, ones = sb("ident", [P, P]), sb("before", [P, P]), sb("ones", [P, P])
        nums = sb("nums", [P, E + TILES])
        gw, gb = sb("gw", [P, DC, E]), sb("gb", [P, E])
        logits = sb("logits", [P, NT, E])
        first, second, both = sb("first", [P, NT, E]), sb("second", [P, NT, E]), sb("both", [P, NT, E])
        work = sb("work", [P, NT, E])
        total, upto, zero = sb("total", [P, E, NT]), sb("upto", [P, E, NT]), sb("zero", [P, E * NT])
        best, pick, next_best = sb("best", [P, NT]), sb("pick", [P, NT]), sb("next_best", [P, NT])
        gap, den = sb("gap", [P, NT]), sb("den", [P, NT])
        wt = sb("wt", [P, TOP, NT])
        slotf, slot = sb("slotf", [P, TOP, NT]), sb("slot", [P, TOP, NT], I32)
        count, tiles_i, tiles_f = sb("count", [P, E]), sb("tiles_i", [P, E], I32), sb("tiles_f", [P, E])
        tiles_upto, base = sb("tiles_upto", [P, E]), sb("base", [P, E])
        passed, owner, owner_i = sb("passed", [P, TILES, E]), sb("owner", [P, TILES]), sb("owner_i", [P, TILES], I32)
        back = sb("back", [P, 4, TOP, D])
        bn, mv = sb("bn2", [P, 2, 6]), sb("mv2", [P, 2, 2])
        var, rstd, minus_half = sb("var2", [P, 2]), sb("rstd2", [P, 2]), sb("minus_half2", [P, 1])
        fin = sb("fin", [P, 4, D])
        ps = ctx.enter_context(nc.psum_tensor("ps2", [P, 8, 512], F32))

        consts_in, minus_set = sem("consts_in2"), sem("minus_set")
        gt_ready, gt_done, lg_ready, lg_done = sem("gt_ready"), sem("gt_done"), sem("lg_ready"), sem("lg_done")
        route_step, gap_done, gap_exp, both_done, ranks_ready, slots_known = (
            sem("route_step"), sem("gap_done"), sem("gap_exp"), sem("both_done"), sem("ranks_ready"), sem("slots_known"))
        sent = sem("sent")
        w1_in, w2_in, b_in, x_in = sem("w1_in"), sem("w2_in"), sem("b_in"), sem("x_in2")
        w_hi, w_lo = sem("w_hi"), sem("w_lo")
        tr_ready, xhi_done, xlo_done = sem("tr_ready"), sem("xhi_done"), sem("xlo_done")
        m1_ready, gelu_done, hhi_done, h_done = sem("m1_ready"), sem("gelu_done"), sem("hhi_done"), sem("h_done")
        y_ready, ysum, y_done, y_out = sem("y_ready"), sem("ysum"), sem("y_done"), sem("y_out")
        back_in = [sem(f"back_in{n}") for n in range(4)]
        c_step, var_done, rstd_done, fin_done = sem("c_step"), sem("var_done2"), sem("rstd_done2"), sem("fin_done")
        fin_out = [sem(f"fin_out{n}") for n in range(4)]

        block = ctx.enter_context(nc.Block())
        CONSTS = 6

        def slots_tile(dram, at):
            return dram.rearrange("s d -> (s d)")[bass.ds(at, TS * D)].rearrange("(p c d) -> p c d", p=P, c=C)


        def is_shared(s):
            return s < HEAD or s >= LAST

        def tokens(s):
            n = (s if s < HEAD else s - TILES) * C
            return range(n, n + C)

        LAG = 4
        LASTS = END - LAST

        @block.sync
        def _(sp):
            def load_w1(src):
                sp.dma_start(w1raw[:, :, :], src).then_inc(w1_in, 16)

            def load_w2(src):
                sp.dma_start(w2raw[:, :, :], src).then_inc(w2_in, 16)

            def load_b(e, u):
                sp.dma_start(bias1[:, u, :], b1[bass.ds(e, 1)].rearrange("e p c -> p (e c)")).then_inc(b_in, 16)
                sp.dma_start(bias2[:, u, :], b2[bass.ds(e, 1), :].to_broadcast([P, D])).then_inc(b_in, 16)

            def w1_of(e):
                return w1[bass.ds(e, 1)].rearrange("e (k p) n -> p (e k) n", p=P)

            def w2_of(e):
                return w2[bass.ds(e, 1)].rearrange("e (c p) n -> p (e c) n", p=P)

            load_w1(w1_of(E))
            load_w2(w2_of(E))
            load_b(E, 1)
            for dst, src in ((ident, masks[:, 1, :]), (before, masks[:, 2, :]), (ones, masks[:, 3, :]),
                             (nums, numbers), (gw, gate_w.rearrange("(k p) e -> p k e", p=P)),
                             (gb, gate_b.rearrange("(a e) -> a e", a=1).to_broadcast([P, E]))):
                sp.dma_start(dst[:], src).then_inc(consts_in, 16)

            def prefetch(s, u, shared_next=False):
                r = s + 1 - HEAD
                at = r * TS * D if isinstance(r, int) else sp.snap(r * (TS * D))
                e = E if shared_next else sp.value_load(owner_i[0:1, bass.ds(r, 1)], min_val=0, max_val=E - 1)
                sp.wait_ge(w_lo, HC * r + HALF)
                load_w1(w1_of(e))
                if not shared_next:
                    sp.wait_ge(x_in, 16 * r)
                    sp.wait_ge(tr_ready, 2 * s)
                    sp.dma_start(rows[:, 1 - u, :, :], slots_tile(slots_in, at)).then_inc(x_in, 16)
                sp.wait_ge(w_lo, HC * r + HC)
                load_w2(w2_of(e))
                sp.wait_ge(y_done, s)
                sp.wait_ge(b_in, 32 * (r + 1))
                load_b(e, 1 - u)
                return r

            def store(s, u):
                r = s - HEAD
                at = r * TS * D if isinstance(r, int) else sp.snap(r * (TS * D))
                sp.wait_ge(y_out, 16 * r + 32)
                sp.wait_ge(y_done, s + 1)
                sp.dma_start(slots_tile(slots_out, at), ys[:, u, :, :]).then_inc(y_out, 16)

            sp.sem_inc(y_out, 32)
            sp.wait_ge(slots_known, 1)
            e = sp.value_load(owner_i[0:1, 0:1], min_val=0, max_val=E - 1)
            sp.wait_ge(w_lo, HALF)
            load_w1(w1_of(e))
            sp.wait_ge(w_lo, HC)
            load_w2(w2_of(e))
            sp.wait_ge(b_in, 32)
            load_b(e, 0)
            sp.wait_ge(sent, 16 * TOP * NT)
            sp.dma_start(rows[:, 0, :, :], slots_tile(slots_in, 0)).then_inc(x_in, 16)
            prefetch(HEAD, 0)
            with sp.Fori(0, (TILES - 3) // 2) as i:
                for u in (1, 0):
                    s = HEAD + 2 * i + (1 if u else 2)
                    prefetch(s, u)
                    store(s - 1, 1 - u)
            prefetch(LAST - 2, 1)
            store(LAST - 3, 0)
            prefetch(LAST - 1, 0, shared_next=True)
            store(LAST - 2, 1)
            store(LAST - 1, 0)
            for t in range(NT):
                sp.wait_ge(fin_done, t + 1)
                sp.dma_start(out[t * P:(t + 1) * P, :], fin[:, t % 4, :]).then_inc(fin_out[t % 4], 16)
            for n in range(4):
                sp.wait_ge(fin_out[n], 16 * NT // 4)

        @block.tensor
        def _(pe):
            pe.wait_ge(consts_in, 16 * CONSTS)
            for q in range(NT // C):
                u = q % 2
                if q >= 2:
                    pe.wait_ge(gt_done, 2 * (q - 1))
                for k in range(DC):
                    for c in range(C):
                        mm = pe.transpose(ps[:, 2 * u + k, c * P:(c + 1) * P],
                                          res[:, C * q + c, k * P:(k + 1) * P], ident[:, :])
                    mm.then_inc(gt_ready, 1)
                pe.wait_ge(gt_done, 2 * (q + 1))
                if q >= 2:
                    pe.wait_ge(lg_done, q - 1)
                for c in range(C):
                    for k in range(DC):
                        mm = pe.matmul(ps[:, 4 + u, c * E:(c + 1) * E], yT[:, u, k, c * P:(c + 1) * P], gw[:, k, :],
                                       start=c == 0 and k == 0, stop=c == C - 1 and k == DC - 1, skip_group_check=True)
                mm.then_inc(lg_ready, 1)
            pe.wait_ge(both_done, 1)
            pe.matmul(ps[:, 0, 0:NT * E], before[:, :], both[:, :, :].rearrange("p t e -> p (t e)"), start=True, stop=True)
            pe.matmul(ps[:, 1, 0:NT * E], ones[:, :], both[:, :, :].rearrange("p t e -> p (t e)"),
                      start=True, stop=True).then_inc(ranks_ready, 1)

            def turn(s, u):
                if not is_shared_now:
                    pe.wait_ge(x_in, 16 * (s - HEAD + 1))
                for k in range(DC):
                    for c in range(C):
                        src = res[:, tokens(s)[c], :] if is_shared_now else rows[:, u, c, :]
                        mm = pe.transpose(ps[:, 6 + k, c * P:(c + 1) * P], src[:, k * P:(k + 1) * P], ident[:, :])
                    mm.then_inc(tr_ready, 1)

            def up(s, u, w, c, load=None):
                if c == 0:
                    pe.wait_ge(xhi_done, 2 * s + 2)
                    pe.wait_ge(xlo_done, 2 * s + 2)
                    if load is not None:
                        pe.wait_ge(w_lo, HC * load + HALF)
                cols = slice(c * P, (c + 1) * P)
                n = 0
                for k in range(DC):
                    for a, b in ((w1hi, xhi), (w1hi, xlo), (w1lo, xhi)):
                        mm = pe.matmul(ps[:, c % 2, :], a[:, w, k, cols], b[:, u, k, :], start=n == 0, stop=n == 3 * DC - 1)
                        n += 1
                mm.then_inc(m1_ready, 1)

            def down(s, u, w, c, load=None):
                if c == 0 and load is not None:
                    pe.wait_ge(w_lo, HC * load + HC)
                pe.wait_ge(h_done, HC * s + c + 1)
                for q in range(C):
                    to = ps[:, 2 + 2 * u + q // 2, (q % 2) * D:(q % 2) * D + D]
                    for n, (a, b) in enumerate(((hhi, w2hi), (hhi, w2lo), (hlo, w2hi))):
                        mm = pe.matmul(to, a[:, c % 2, q * P:(q + 1) * P], b[:, w, c, :],
                                       start=c == 0 and n == 0 and q % 2 == 0, stop=c == HC - 1 and n == 2,
                                       skip_group_check=True)
                if c == HC - 1:
                    mm.then_inc(y_ready, 1)

            def tile(s, u, w, load, nxt):
                nonlocal is_shared_now
                for c in range(HC):
                    if c < HC - 1:
                        up(s, u, w, c + 1)
                    elif nxt:
                        up(s + 1, nxt[0], nxt[1], 0, nxt[2])
                    down(s, u, w, c, load)
                    if c == 3 and nxt:
                        is_shared_now = nxt[3]
                        turn(s + 1, nxt[0])

            is_shared_now = True
            turn(0, 0)
            up(0, 0, 1, 0, 0)
            for s in range(HEAD):
                tile(s, s % 2, 1, 0, ((s + 1) % 2, 1, 0, True) if s < HEAD - 1 else (0, 0, 1, False))
            with pe.Fori(0, (TILES - 1) // 2) as i:
                for u in range(2):
                    s, load = HEAD + 2 * i + u, 2 * i + u + 1
                    tile(s, u, u, load, (1 - u, 1 - u, load + 1, False))
            tile(LAST - 1, 0, 0, TILES, (1, 1, TILES + 1, True))
            for s in range(LAST, END):
                tile(s, s % 2, 1, TILES + 1, ((s + 1) % 2, 1, TILES + 1, True) if s < END - 1 else None)

        def split(eng, load, w, c, lo):
            if c < HALF:
                k, cols = c // 2, slice((c % 2) * 512, (c % 2) * 512 + 512)
                raw, hi, low = w1raw[:, k, cols], w1hi[:, w, k, cols], w1lo[:, w, k, cols]
            else:
                n = 2 * (c - HALF)
                raw, hi, low = w2raw[:, n:n + 2, :], w2hi[:, w, n:n + 2, :], w2lo[:, w, n:n + 2, :]
            if lo:
                eng.wait_ge(w_hi, HC * load + c + 1)
                eng.tensor_tensor(low, raw, hi.bitcast(F32), ALU.subtract).then_inc(w_lo, 1)
            else:
                if c == 0:
                    eng.wait_ge(w1_in, 16 * (load + 1))
                if c == HALF:
                    eng.wait_ge(w2_in, 16 * (load + 1))
                eng.activation(hi, raw, ACT.Copy).then_inc(w_hi, 1)

        @block.scalar
        def _(act):
            for q in range(NT // C):
                act.wait_ge(gt_ready, 2 * q + 2)
                if q >= 2:
                    act.wait_ge(lg_ready, q - 1)
                act.activation(yT[:, q % 2, 0, :], ps[:, 2 * (q % 2), :], ACT.Copy).then_inc(gt_done, 1)
                act.activation(yT[:, q % 2, 1, :], ps[:, 2 * (q % 2) + 1, :], ACT.Copy).then_inc(gt_done, 1)
            act.wait_ge(gap_done, 1)
            act.activation(gap[:, :], gap[:, :], ACT.Exp).then_inc(gap_exp, 1)
            for c in range(HC):
                split(act, 0, 1, c, False)

            def turned(s, u):
                for k in range(DC):
                    act.wait_ge(tr_ready, 2 * s + k + 1)
                    act.activation(xhi[:, u, k, :], ps[:, 6 + k, :], ACT.Copy).then_inc(xhi_done, 1)

            def tile(s, u, w, nxt=None, load=None):
                for c in range(HC):
                    act.wait_ge(m1_ready, HC * s + c + 1)
                    if c == 0:
                        act.wait_ge(b_in, 32 * bias_loads)
                    act.activation(h[:, c % 2, :], ps[:, c % 2, :], ACT.Gelu, bias=bias1[:, w, c:c + 1]).then_inc(gelu_done, 1)
                    if c == 4 and nxt:
                        turned(s + 1, 1 - u)
                    if load is not None:
                        if c == 0:
                            act.wait_ge(y_ready, s)
                        split(act, load[0], load[1], c, False)

            turned(0, 0)
            for s in range(HEAD):
                bias_loads = 1
                tile(s, s % 2, 1, True, (1, 0) if s == HEAD - 1 else None)
            with act.Fori(0, (TILES - 1) // 2) as i:
                for u in range(2):
                    bias_loads = 2 * i + u + 2
                    tile(HEAD + 2 * i + u, u, u, True, (2 * i + u + 2, 1 - u))
            bias_loads = TILES + 1
            tile(LAST - 1, 0, 0, True, (TILES + 1, 1))
            bias_loads = TILES + 2
            for s in range(LAST, END):
                tile(s, s % 2, 1, s < END - 1)

        @block.gpsimd
        def _(pool):
            pool.memset(minus_half[:, :], -0.5).then_inc(minus_set, 1)
            pool.wait_ge(minus_set, 1)
            pool.wait_ge(slots_known, 1)
            for t in range(NT):
                for n in range(TOP):
                    pool.indirect_dma_start(slots_in, bass.IndirectOffsetOnAxis(ap=slot[:, n, t:t + 1], axis=0),
                                            res[:, t, :], None).then_inc(sent, 16)
                if t % C == C - 1:
                    pool.wait_ge(sent, 16 * TOP * (t + 1))

            def fetch(t):
                if t >= 4:
                    pool.wait_ge(c_step, 4 * (t - 4) + 2)
                for n in range(TOP):
                    pool.indirect_dma_start(back[:, t % 4, n, :], None, slots_out,
                                            bass.IndirectOffsetOnAxis(ap=slot[:, n, t:t + 1], axis=0)).then_inc(back_in[t % 4], 16)

            def root(t):
                pool.wait_ge(var_done, t + 1)
                pool.tensor_tensor(rstd[:, t % 2:t % 2 + 1], var[:, t % 2:t % 2 + 1], minus_half[:, :], ALU.pow).then_inc(rstd_done, 1)

            pool.wait_ge(y_out, 16 * TILES + 32)
            for t in range(NT + 4):
                if t < NT:
                    fetch(t)
                if t >= 4:
                    root(t - 4)

        @block.vector
        def _(dve):
            steps = 0

            def step(ins):
                nonlocal steps
                ins.then_inc(route_step, 1)
                steps += 1
                dve.wait_ge(route_step, steps)

            def over(ap, n):
                return ap.unsqueeze(2).to_broadcast([P, ap.shape[1], n])

            def across(ap, n):
                return ap.unsqueeze(1).to_broadcast([P, n, ap.shape[1]])

            dve.wait_ge(consts_in, 16 * CONSTS)
            for q in range(NT // C):
                dve.wait_ge(lg_ready, q + 1)
                dve.tensor_tensor(logits[:, C * q:C * (q + 1), :],
                                  ps[:, 4 + q % 2, 0:C * E].rearrange("p (c e) -> p c e", c=C),
                                  across(gb[:, :], C), ALU.add).then_inc(lg_done, 1)
            dve.wait_ge(lg_done, NT // C)
            rev = across(nums[:, 0:E], NT)

            def choose(values, top, into):
                step(dve.tensor_reduce(top[:, :], values[:, :, :], AX_X, ALU.max))
                step(dve.tensor_tensor(work[:, :, :], values[:, :, :], over(top[:, :], E), ALU.is_equal))
                step(dve.tensor_tensor(work[:, :, :], work[:, :, :], rev, ALU.mult))
                step(dve.tensor_reduce(pick[:, :], work[:, :, :], AX_X, ALU.max))
                step(dve.tensor_tensor(into[:, :, :], work[:, :, :], over(pick[:, :], E), ALU.is_equal))

            choose(logits, best, first)
            step(dve.scalar_tensor_tensor(both[:, :, :], first[:, :, :], -3.0e38, logits[:, :, :], ALU.mult, ALU.add))
            choose(both, next_best, second)
            step(dve.tensor_tensor(gap[:, :], next_best[:, :], best[:, :], ALU.subtract))
            dve.tensor_tensor(both[:, :, :], first[:, :, :], second[:, :, :], ALU.add).then_inc(both_done, 1)
            dve.sem_inc(gap_done, 1)
            dve.wait_ge(gap_exp, 1)
            step(dve.tensor_scalar(den[:, :], gap[:, :], 1.0, None, ALU.add))
            step(dve.reciprocal(wt[:, 0, :], den[:, :]))
            step(dve.tensor_tensor(wt[:, 1, :], gap[:, :], wt[:, 0, :], ALU.mult))
            step(dve.memset(zero[:, :], 0.0))
            dve.wait_ge(ranks_ready, 1)
            step(dve.tensor_copy(total[:, :, :], ps[:, 1, 0:NT * E].rearrange("p (t e) -> p e t", e=E)))
            step(dve.tensor_tensor_scan(upto[:, :, :].rearrange("p e t -> p (e t)"), total[:, :, :].rearrange("p e t -> p (e t)"),
                                        zero[:, :], 0.0, ALU.add, ALU.add))
            step(dve.tensor_tensor(total[:, :, :], upto[:, :, :], total[:, :, :], ALU.subtract))
            step(dve.tensor_tensor(count[:, :], upto[:, :, NT - 1], total[:, :, 0], ALU.subtract))
            step(dve.tensor_scalar(tiles_i[:, :], count[:, :], float(TS - 1), None, ALU.add))
            step(dve.tensor_scalar(tiles_i[:, :], tiles_i[:, :], TS.bit_length() - 1, None, ALU.arith_shift_right))
            step(dve.tensor_copy(tiles_f[:, :], tiles_i[:, :]))
            step(dve.tensor_tensor_scan(tiles_upto[:, :], tiles_f[:, :], zero[:, 0:E], 0.0, ALU.add, ALU.add))
            step(dve.tensor_tensor(base[:, :], tiles_upto[:, :], tiles_f[:, :], ALU.subtract))
            step(dve.scalar_tensor_tensor(base[:, :], base[:, :], float(TS), total[:, :, 0], ALU.mult, ALU.subtract))
            step(dve.tensor_tensor(total[:, :, :], total[:, :, :], over(base[:, :], NT), ALU.add))
            step(dve.tensor_tensor(work[:, :, :], ps[:, 0, 0:NT * E].rearrange("p (t e) -> p t e", e=E),
                                   total[:, :, :].rearrange("p e t -> p t e"), ALU.add))
            for n, hot in enumerate((first, second)):
                step(dve.tensor_tensor(hot[:, :, :], hot[:, :, :], work[:, :, :], ALU.mult))
                step(dve.tensor_reduce(slotf[:, n, :], hot[:, :, :], AX_X, ALU.add))
            step(dve.tensor_copy(slot[:, :, :], slotf[:, :, :]))
            step(dve.tensor_tensor(passed[:, :, :], across(tiles_upto[:, :], TILES), over(nums[:, E:], E), ALU.is_le))
            step(dve.tensor_reduce(owner[:, :], passed[:, :, :], AX_X, ALU.add))
            dve.tensor_scalar(owner_i[:, :], owner[:, :], float(E - 1), None, ALU.min).then_inc(slots_known, 1)

            for c in range(HC):
                split(dve, 0, 1, c, True)

            def turned(s, u):
                for k in range(DC):
                    dve.wait_ge(xhi_done, 2 * s + k + 1)
                    dve.tensor_tensor(xlo[:, u, k, :], ps[:, 6 + k, :], xhi[:, u, k, :].bitcast(F32), ALU.subtract).then_inc(xlo_done, 1)

            def halve(s, c):
                dve.wait_ge(gelu_done, HC * s + c + 1)
                dve.tensor_copy(hhi[:, c % 2, :], h[:, c % 2, :]).then_inc(hhi_done, 1)
                dve.wait_ge(hhi_done, HC * s + c + 1)
                dve.tensor_tensor(hlo[:, c % 2, :], h[:, c % 2, :], hhi[:, c % 2, :].bitcast(F32), ALU.subtract).then_inc(h_done, 1)

            def collect(s, u, w):
                dve.wait_ge(y_ready, s + 1)
                if is_shared_now:
                    if s < HEAD:
                        dve.wait_ge(sent, 16 * TOP * C * (s + 1))
                else:
                    dve.wait_ge(y_out, 16 * (s - HEAD) + 16)
                for a in range(2):
                    ins = dve.tensor_tensor(ys[:, u, 2 * a:2 * a + 2, :],
                                            ps[:, 2 + 2 * u + a, :].rearrange("p (c d) -> p c d", c=2),
                                            bias2[:, w, :].unsqueeze(1).to_broadcast([P, 2, D]), ALU.add)
                if not is_shared_now:
                    ins.then_inc(y_done, 1)
                else:
                    t = tokens(s)
                    n = s if s < HEAD else s - TILES
                    ins.then_inc(ysum, 1)
                    dve.wait_ge(ysum, n + 1)
                    dve.tensor_tensor(res[:, t[0]:t[-1] + 1, :], res[:, t[0]:t[-1] + 1, :], ys[:, u, :, :], ALU.add).then_inc(y_done, 1)

            done = 0

            def mix(t):
                nonlocal done
                g = t % 4
                shared = t // C if t // C < HEAD else t // C + TILES
                dve.wait_ge(y_done, shared + 1)
                dve.wait_ge(back_in[g], 32 * (t // 4 + 1))
                for n in range(TOP):
                    dve.scalar_tensor_tensor(res[:, t, :], back[:, g, n, :], wt[:, n, t:t + 1], res[:, t, :],
                                             ALU.mult, ALU.add).then_inc(c_step, 1)
                    done += 1
                    dve.wait_ge(c_step, done)
                dve.bn_stats(bn[:, t % 2, :], res[:, t, :]).then_inc(c_step, 1)
                dve.wait_ge(c_step, done + 1)
                dve.bn_aggr(mv[:, t % 2, :], bn[:, t % 2, :]).then_inc(c_step, 1)
                done += 2
                dve.wait_ge(c_step, done)
                dve.tensor_scalar(var[:, t % 2:t % 2 + 1], mv[:, t % 2, 1:2], EPS, None, ALU.add).then_inc(var_done, 1)

            def finish(t):
                dve.wait_ge(rstd_done, t + 1)
                if t >= 4:
                    dve.wait_ge(fin_out[t % 4], 16 * (t // 4))
                dve.tensor_scalar(fin[:, t % 4, :], res[:, t, :], mv[:, t % 2, 0:1], rstd[:, t % 2:t % 2 + 1],
                                  ALU.subtract, ALU.mult).then_inc(fin_done, 1)

            def combine(n):
                if 0 <= n < NT:
                    mix(n)
                if 0 <= n - 1 < NT:
                    finish(n - 1)

            def tile(s, u, w, nxt=True, load=None, at=None):
                for c in range(HC):
                    if c < HC - 1:
                        halve(s, c + 1)
                    elif nxt:
                        halve(s + 1, 0)
                    if load is not None:
                        split(dve, load[0], load[1], c, True)
                    if c == 4 and nxt:
                        turned(s + 1, 1 - u)
                    if at is not None:
                        combine(at + c - LAG)
                collect(s, u, w)

            turned(0, 0)
            halve(0, 0)
            is_shared_now = True
            for s in range(HEAD):
                tile(s, s % 2, 1, True, (1, 0) if s == HEAD - 1 else None)
            is_shared_now = False
            with dve.Fori(0, (TILES - 1) // 2) as i:
                for u in range(2):
                    tile(HEAD + 2 * i + u, u, u, True, (2 * i + u + 2, 1 - u))
            tile(LAST - 1, 0, 0, True, (TILES + 1, 1))
            is_shared_now = True
            for s in range(LAST, END):
                tile(s, s % 2, 1, s < END - 1, None, HC * (s - LAST))
            for n in range(HC * LASTS - LAG, NT + 1):
                combine(n)


def host_constants():
    inv = np.float32(10000.0) ** (-np.arange(0, DR, 2, dtype=np.float32) / np.float32(DR))
    ang = np.arange(S, dtype=np.float32)[:, None] * inv
    rope = np.zeros((P, 2, S), np.float32)
    rope[:, 0, :] = 1.0
    for i in range(HG):
        for r in range(DR):
            row = SLOT * i + DH + r
            rope[row, 0] = np.cos(ang[:, r // 2])
            rope[row, 1] = np.sin(ang[:, r // 2]) * (-1.0 if r % 2 == 0 else 1.0)
    masks = np.zeros((P, 5, P), np.float32)
    for i in range(HG):
        for d in range(DH):
            masks[SLOT * i + d, 0, DH * i + d] = 1.0
        masks[SLOT * i + DH, 0, HG * DH + i] = 1.0
    masks[:, 1, :] = np.eye(P)
    masks[:, 2, :] = np.triu(np.ones((P, P)), 1)
    masks[:, 3, :] = 1.0
    masks[:, 4, :] = np.triu(np.ones((P, P)))
    numbers = np.zeros((P, E + TILES), np.float32)
    numbers[:, :E] = E - np.arange(E)
    numbers[:, E:] = np.arange(TILES)
    return rope, masks, numbers


def attention_layouts(x, W_DQ, W_UQ, W_QR, W_DKV, W_UK, W_UV, W_KR, W_O):
    xf = x.reshape(T, D)
    x_tok = np.ascontiguousarray(xf.reshape(NT, P, D).transpose(1, 0, 2))
    x_t = np.ascontiguousarray(xf.T.reshape(DC, P, T).transpose(1, 0, 2))
    w_down = np.concatenate([W_DQ, W_DKV], axis=1).reshape(DC, P, 2 * LAT).transpose(1, 0, 2)
    partner = np.arange(DR) ^ 1
    w_q = np.zeros((LAT, 2, H, SLOT), np.float32)
    w_q[:, 0, :, :DH] = W_UQ.reshape(LAT, H, DH)
    w_q[:, 0, :, DH:DH + DR] = W_QR.reshape(LAT, H, DR)
    w_q[:, 1, :, DH:DH + DR] = W_QR.reshape(LAT, H, DR)[:, :, partner]
    w_q = w_q.reshape(LAT, 2, G, P).transpose(0, 2, 1, 3)
    w_k = np.zeros((LAT, H, SLOT), np.float32)
    w_k[:, :, :DH] = W_UK.reshape(LAT, H, DH)
    w_kv = np.concatenate([w_k.reshape(LAT, G * P), W_UV], axis=1)
    w_kr = np.zeros((D, 2, HG, SLOT), np.float32)
    w_kr[:, 0, :, DH:DH + DR] = W_KR[:, None, :]
    w_kr[:, 1, :, DH:DH + DR] = W_KR[:, None, partner]
    w_kr = w_kr.reshape(DC, P, 2, P).transpose(1, 0, 2, 3)
    w_o = W_O.reshape(DC, P, D).transpose(1, 0, 2)
    return [np.ascontiguousarray(a) for a in (x_tok, x_t, w_down, w_q, w_kv, w_kr, w_o)]


def build(nc, x, xT, w_down, w_q, w_kv, w_kr, w_o, w1, w2, b1, b2, gate_w, gate_b, rope, masks, numbers, out):
    slots_in = nc.dram_tensor("slots_in", (SLOTS, D), F32, kind="Internal").ap()
    slots_out = nc.dram_tensor("slots_out", (SLOTS, D), F32, kind="Internal").ap()
    with nc.sbuf_tensor("res", [P, NT, D], F32) as res:
        attention(nc, x, xT, w_down, w_q, w_kv, w_kr, w_o, rope, masks, res, slots_in)
        experts(nc, res, slots_in, slots_out, w1, w2, b1, b2, gate_w, gate_b, masks, numbers, out)


_INS = ["x", "xT", "w_down", "w_q", "w_kv", "w_kr", "w_o", "w1", "w2", "b1", "b2", "gate_w", "gate_b",
        "rope", "masks", "numbers"]


def kernel(L0_attn_x, L0_attn_W_DQ, L0_attn_W_UQ, L0_attn_W_QR, L0_attn_W_DKV, L0_attn_W_UK, L0_attn_W_UV,
           L0_attn_W_KR, L0_attn_W_O, L0_ffn_gate_w, L0_ffn_gate_b, L0_ffn_w1, L0_ffn_b1, L0_ffn_w2, L0_ffn_b2,
           L0_ffn_ws1, L0_ffn_bs1, L0_ffn_ws2, L0_ffn_bs2):
    import concourse.bacc as bacc
    from concourse.bass_utils import run_bass_kernel_spmd

    a = lambda v: np.asarray(v)
    laid = attention_layouts(a(L0_attn_x), a(L0_attn_W_DQ), a(L0_attn_W_UQ), a(L0_attn_W_QR), a(L0_attn_W_DKV),
                             a(L0_attn_W_UK), a(L0_attn_W_UV), a(L0_attn_W_KR), a(L0_attn_W_O))
    w1 = np.concatenate([a(L0_ffn_w1), a(L0_ffn_ws1)[None]])
    w2 = np.concatenate([a(L0_ffn_w2), a(L0_ffn_ws2)[None]])
    b1 = np.concatenate([a(L0_ffn_b1), a(L0_ffn_bs1)[None]]).reshape(E + 1, HID // P, P).transpose(0, 2, 1)
    b2 = np.concatenate([a(L0_ffn_b2), a(L0_ffn_bs2)[None]])
    arrays = dict(zip(_INS, laid + [w1, w2, b1, b2, a(L0_ffn_gate_w), a(L0_ffn_gate_b), *host_constants()]))
    arrays = {n: np.ascontiguousarray(v) for n, v in arrays.items()}
    nc = bacc.Bacc("TRN2", target_bir_lowering=False, num_devices=1)
    aps = [nc.dram_tensor(n, v.shape, mybir.dt.from_np(v.dtype), kind="ExternalInput").ap() for n, v in arrays.items()]
    out = nc.dram_tensor("out", (T, D), F32, kind="ExternalOutput").ap()
    build(nc, *aps, out)
    r = run_bass_kernel_spmd(nc, [arrays], core_ids=[0])
    return r.results[0]["out"].reshape(B, S, D)
```

```python
from contextlib import ExitStack

import numpy as np
import concourse.bass as bass
from concourse import mybir

F32 = mybir.dt.float32
F32R = mybir.dt.float32r
I32 = mybir.dt.int32
ALU = mybir.AluOpType
ACT = mybir.ActivationFunctionType
AX_X = mybir.AxisListType.X

P = 128
B, S, D = 8, 512, 256
T = B * S
NT = T // P
H, DH, DR = 16, 16, 8
LAT = 64
SLOT = 32
HG = P // SLOT
G = H // HG
KB = S // P
DC = D // P
SCALE = 1.0 / float(np.sqrt(np.float32(DH + DR)))
E, HID = 8, 1024
TOP = 2
TS = 512
TILES = TOP * T // TS + E - 1
SLOTS = TILES * TS
GATED = 6
CLIP = 80.0
EPS = 1e-5

COLS = [S - P * j for j in range(KB)]
AT = [0, S, 2 * S, S + COLS[1]]
EW = sum(COLS)
SCORE_AT = [0, S, 3 * S - COLS[2], 2 * S]
SCORE_FROM = [0, P, 2 * P, 2 * P]
PARTS = 3
AHEAD = 3


def attention(nc, x, xT, w_down, w_q, w_kv, w_kr, w_o, rope, masks, gate_w, gate_b, res, ident, gw, gb, logits,
              slots_in):
    C_AT, KR_AT, FLIP_AT, KRB_AT, V_AT = 0, 1, 3, 2, 15
    QA_AT, QB_AT, KK_AT = {5: 0, 6: 1, 8: 2, 10: 3}, {5: 0, 7: 1, 8: 2, 10: 3}, {5: 0, 7: 1, 8: 2, 10: 3}
    HIGH_AT, LOW_AT = {6: (0,), 8: (1,), 15: (2, 3)}, {6: (0,), 8: (1,), 15: (2, 3)}
    O_AT = {12: 0, 14: 1}
    TURN_AT = {0: 0, 1: 1, 4: 2, 6: 3, 8: 4, 10: 5}
    GATE_AT = {1: 0, 3: 1, 5: 2, 7: 3, 9: 4, 11: 5}
    BACK_AT = {2: 0, 4: 1, 6: 2, 8: 3, 10: 4, 12: 5}
    PLACE_AT = {0: 1, 1: 2, 2: 3}

    with ExitStack() as ctx:
        def sb(name, shape, dt=F32):
            return ctx.enter_context(nc.sbuf_tensor(name, shape, dt))

        def sem(name):
            return ctx.enter_context(nc.semaphore(name))

        xt = sb("xt", [P, DC, S])
        wd = sb("wd", [P, DC, 2 * LAT])
        QW = G * 2 * P
        KW = G * P + D
        wq2, wkv2 = sb("wq2", [P, QW], F32R), sb("wkv2", [P, KW], F32R)
        wlo = sb("wlo", [P, QW], F32R)
        wkr = sb("wkr", [P, DC, 2, P])
        wo = sb("wo", [P, DC, D])
        cs = sb("cs", [P, 2, S])
        pick = sb("slot_pick", [P, P])
        c2 = sb("c2", [P, 2, S], F32R)
        clo = sb("clo", [P, S], F32R)
        kr = sb("kr", [P, S])
        sinpart = sb("sinpart", [P, 2, S])
        krsin = sinpart[:, 1, :]
        qt, kt = sb("qt", [P, 2, S]), sb("kt", [P, 2, S])
        qhi, qlo, khi, klo = (sb(n, [P, 2, S], F32R) for n in ("qhi", "qlo", "khi", "klo"))
        qs, ks = sb("qs", [PARTS * SLOT, H, S], F32R), sb("ks", [PARTS * SLOT, H, S], F32R)
        v = sb("v", [P, KB, H, SLOT])
        vnext = sb("vnext", [P, KB, H, DH])
        e = sb("e", [P, 4, EW])
        ot = sb("ot", [P, 2, S])
        rec = sb("rec", [P, 2, KB, HG])
        onq = sb("onq", [P, KB, H * DH])
        on = sb("on", [P, DC, S])
        bn = sb("bn", [P, KB, 6])
        mv = sb("mv", [P, KB, 2])
        var = sb("var", [P, KB])
        rstd = sb("rstd", [P, KB])
        minus_half = sb("minus_half", [P, KB])
        row = sb("row", [P, KB, D])
        causal = sb("causal", [P, 1, P])
        zeros = xt[:, 0:1, 0:D]
        ps = ctx.enter_context(nc.psum_tensor("ps", [P, 8, S], F32))
        SC, PROJ, PV = 0, 3, 6

        consts_in, down_in = sem("consts_in"), sem("down_in")
        xt_in, rows_in = sem("xt_in"), sem("rows_in")
        ones_set = sem("ones_set")
        c_ready, chi_done, clo_done, c_stacked = sem("c_ready"), sem("chi_done"), sem("clo_done"), sem("c_stacked")
        whi_done, wlo_done = sem("whi_done"), sem("wlo_done")
        kr_ready, kr_steps = sem("kr_ready"), sem("kr_steps")
        v_ready, v_done, v_placed = sem("v_ready"), sem("v_done"), sem("v_placed")
        q_ready, k_ready, q_done = sem("q_ready"), sem("k_ready"), sem("q_done")
        q_read, partners_read, k_read = sem("q_read"), sem("partners_read"), sem("k_read")
        hi_done, lo_done = sem("hi_done"), sem("lo_done")
        stacked = [sem(f"stacked{i}") for i in range(HG)]
        s01_ready, exp01_done = sem("s01_ready"), sem("exp01_done")
        s_ready, exp_done, clip_done, mask_done = sem("s_ready"), sem("exp_done"), sem("clip_done"), sem("mask_done")
        pv_done, ot_done, turned, rec_done, normed = sem("pv_done"), sem("ot_done"), sem("turned"), sem("rec_done"), sem("normed")
        flipped, on_done = sem("flipped"), sem("on_done")
        a_ready, res_done, bn_done, mv_done = sem("a_ready"), sem("res_done"), sem("bn_done"), sem("mv_done")
        var_done, rstd_done = sem("var_done"), sem("rstd_done")
        rows_done = sem("rows_done")
        gt_ready, gt_done, lt_ready, lt_done, lg_ready, lg_done = (
            sem(n) for n in ("gt_ready1", "gt_done1", "lt_ready1", "lt_done1", "lg_ready1", "lg_done1"))
        zeros_set, slots_zeroed = sem("zeros_set"), sem("slots_zeroed")

        block = ctx.enter_context(nc.Block())
        CONSTS = 11
        turned_rows = (qt, kt)
        lt = sinpart
        PICKED = HG * (DH + 1)
        STACK = 16 * 2 * PARTS

        @block.sync
        def _(sp):
            def load_xt(b):
                sp.dma_start(xt[:, :, :], xT[:, :, bass.ds(b * S, S)]).then_inc(xt_in, 16)

            def stack(b, pair, first=False):
                last = G * b + 2 * pair + 1
                if not first:
                    sp.wait_ge(s_ready, H * (b - 1) + 2 * HG * (pair + 1))
                sp.wait_ge(hi_done, 2 * last + 2)
                sp.wait_ge(lo_done, 2 * last + 2)
                for i in range(HG):
                    heads = slice(2 * HG * pair + i, 2 * HG * pair + HG + i + 1, HG)
                    for dst, parts in ((qs, (qhi, qlo, qhi)), (ks, (khi, khi, klo))):
                        for r, src in enumerate(parts):
                            sp.dma_start(dst[SLOT * r:SLOT * (r + 1), heads, :].bitcast(F32),
                                         src[SLOT * i:SLOT * (i + 1), :, :].bitcast(F32)).then_inc(stacked[i], 16)

            def load_rows(b):
                sp.dma_start(res[:, bass.ds(b * KB, KB), :], x[:, bass.ds(b * KB, KB), :]).then_inc(rows_in, 16)

            def batch(b, load):
                if load:
                    sp.wait_ge(kr_ready, 2 * b + 4)
                    load_xt(b + 2)
                stack(b + 1, 0)
                sp.wait_ge(rows_in, 16 * (b + 1))
                load_rows(b + 1)
                stack(b + 1, 1)

            sp.dma_start(xt[:, :, :], xT[:, :, 0:S]).then_inc(xt_in, 16)
            sp.dma_start(wd[:], w_down).then_inc(down_in, 16)
            sp.dma_start(wkr[:], w_kr).then_inc(down_in, 16)
            sp.dma_start(cs[:], rope).then_inc(consts_in, 16)
            for half in (slice(0, LAT), slice(LAT, P)):
                sp.dma_start(e[half, 0, 0:QW], w_q.rearrange("l g r p -> l (g r p)")).then_inc(consts_in, 16)
                sp.dma_start(e[half, 1, 0:KW], w_kv).then_inc(consts_in, 16)
            sp.dma_start(causal[:, 0, :], masks[:, 4, :]).then_inc(consts_in, 16)
            sp.dma_start(pick[:], masks[:, 0, :]).then_inc(consts_in, 16)
            sp.dma_start(ident[:], masks[:, 1, :]).then_inc(consts_in, 16)
            sp.dma_start(wo[:], w_o).then_inc(consts_in, 16)
            sp.dma_start(gw[:], gate_w.rearrange("(k p) e -> p k e", p=P)).then_inc(consts_in, 16)
            sp.dma_start(gb[:], gate_b.rearrange("(a e) -> a e", a=1).to_broadcast([P, E])).then_inc(consts_in, 16)
            sp.wait_ge(kr_ready, 2)
            load_xt(1)
            for pair in range(2):
                stack(0, pair, first=True)
            load_rows(0)
            with sp.Fori(0, B - 2) as b:
                batch(b, True)
            batch(B - 2, False)
            sp.wait_ge(zeros_set, 1)
            with sp.Fori(0, TILES) as n:
                sp.dma_start(slots_in[bass.ds(n * TS, TS), :].rearrange("(p c) d -> p c d", p=P),
                             zeros.to_broadcast([P, TS // P, D])).then_inc(slots_zeroed, 16)
            sp.wait_ge(slots_zeroed, 16 * TILES)
            sp.wait_ge(xt_in, 16 * B)
            sp.wait_ge(rows_in, 16 * B)

        @block.tensor
        def _(pe):
            def latents(b):
                pe.wait_ge(xt_in, 16 * (b + 1))
                for k in range(DC):
                    mm = pe.matmul(ps[:, PROJ, :], wd[:, k, :], xt[:, k, :], start=k == 0, stop=k == DC - 1)
                mm.then_inc(c_ready, 1)

            def rotary_keys(b, r):
                for k in range(DC):
                    mm = pe.matmul(ps[:, PROJ + 1 + r, :], wkr[:, k, r, :], xt[:, k, :],
                                   start=k == 0, stop=k == DC - 1)
                mm.then_inc(kr_ready, 1)

            def values(b):
                pe.wait_ge(c_stacked, 32 * (b + 1))
                for t in range(KB):
                    to, tokens = ps[:, PROJ + 1 + t // 2, (t % 2) * D:(t % 2) * D + D], slice(t * P, (t + 1) * P)
                    pe.matmul(to, c2[:, 1, tokens], wkv2[:, G * P:], start=True, stop=False)
                    mm = pe.matmul(to, c2[LAT:P, 1, tokens], wlo[LAT:P, G * P:KW], start=False, stop=True)
                    if t % 2:
                        mm.then_inc(v_ready, 1)

            def queries(b, g, r=0):
                if g and r == 0:
                    pe.wait_ge(q_read, G * b + g)
                cols = slice((2 * g + r) * P, (2 * g + r + 1) * P)
                pe.matmul(ps[:, PROJ + r, :], wq2[:, cols], c2[:, 0, :], start=True, stop=False)
                pe.matmul(ps[:, PROJ + r, :], wlo[0:LAT, cols], c2[0:LAT, 0, :],
                          start=False, stop=True).then_inc(q_ready, 1)

            def partners(b, g):
                if g:
                    pe.wait_ge(partners_read, G * b + g)
                queries(b, g, 1)

            def keys(b, g):
                if g:
                    pe.wait_ge(k_read, G * b + g)
                cols = slice(g * P, (g + 1) * P)
                pe.matmul(ps[:, PROJ + 2, :], wkv2[:, cols], c2[:, 1, :], start=True, stop=False)
                pe.matmul(ps[:, PROJ + 2, :], wlo[LAT:P, cols], c2[LAT:P, 1, :],
                          start=False, stop=True).then_inc(k_ready, 1)

            def scores(b, h, first=False):
                if h % (2 * HG) < HG:
                    pe.wait_ge(stacked[h % HG], STACK * (2 * b + h // (2 * HG) + 1))
                for j in range(KB):
                    if j % 2 == 0 and not first:
                        pe.wait_ge(exp_done if j else exp01_done, H * b + h)
                    bank, col = SC + SCORE_AT[j] // S, SCORE_AT[j] % S
                    mm = pe.matmul(ps[:, bank, col:col + S - SCORE_FROM[j]], ks[:, h, P * j:P * (j + 1)],
                                   qs[:, h, SCORE_FROM[j]:], start=True, stop=True)
                    if j % 2:
                        mm.then_inc(s_ready if j == 3 else s01_ready, 1)

            def weigh(b, h, first=False):
                g, i = h // HG, h % HG
                if i == 0:
                    pe.wait_ge(v_placed, G * b + g + 1)
                    if not (first and g < 2):
                        pe.wait_ge(normed, G * b + g - 1)
                pe.wait_ge(mask_done, H * b + h + 1)
                for j in range(KB):
                    mm = pe.matmul(ps[SLOT * i:SLOT * (i + 1), PV + g % 2, P * j:], v[:, j, h, :],
                                   e[:, h % 4, AT[j]:AT[j] + COLS[j]], start=j == 0, stop=j == KB - 1)
                mm.then_inc(pv_done, 1)

            def turn(b, g):
                pe.wait_ge(ot_done, G * b + g + 1)
                for t in range(KB):
                    mm = pe.matmul(ps[:, PV + g % 2, t * PICKED:(t + 1) * PICKED], ot[:, g % 2, t * P:(t + 1) * P],
                                   pick[:, 0:PICKED], start=True, stop=True)
                mm.then_inc(turned, 1)

            def flip(b):
                pe.wait_ge(normed, G * (b + 1))
                for c in range(DC):
                    for t in range(KB):
                        mm = pe.matmul(ps[:, PROJ + c, t * P:(t + 1) * P], onq[:, t, c * P:(c + 1) * P], ident[:, :],
                                       start=True, stop=True)
                    mm.then_inc(flipped, 1)

            def output(b, half):
                pe.wait_ge(on_done, DC * (b + 1))
                bank = PROJ + (0 if half else 2)
                for t in range(2 * half, 2 * half + 2):
                    for c in range(DC):
                        mm = pe.matmul(ps[:, bank, (t % 2) * D:(t % 2) * D + D], on[:, c, t * P:(t + 1) * P],
                                       wo[:, c, :], start=c == 0, stop=c == DC - 1)
                mm.then_inc(a_ready, 1)

            def turn_rows(q):
                pe.wait_ge(rows_done, q + 1)
                if q == 0:
                    pe.wait_ge(q_read, G * B)
                    pe.wait_ge(v_done, 2 * B)
                elif q == 2:
                    pe.wait_ge(on_done, DC * (B - 1))
                else:
                    pe.wait_ge(gt_done, DC * q)
                for k in range(DC):
                    for t in range(KB):
                        mm = pe.transpose(ps[:, PROJ + k, t * P:(t + 1) * P], res[:, KB * q + t, k * P:(k + 1) * P],
                                          ident[:, :])
                    mm.then_inc(gt_ready, 1)

            def gate(q):
                pe.wait_ge(gt_done, DC * (q + 1))
                if q:
                    pe.wait_ge(lg_done, q)
                for k in range(DC):
                    mm = pe.matmul(ps[0:E, PROJ + 2, :], gw[:, k, :], turned_rows[q % 2][:, k, :],
                                   start=k == 0, stop=k == DC - 1)
                mm.then_inc(lt_ready, 1)

            def turn_back(q):
                pe.wait_ge(lt_done, q + 1)
                for t in range(KB):
                    mm = pe.transpose(ps[:, PROJ + 2, t * E:(t + 1) * E], lt[0:E, q % 2, t * P:(t + 1) * P], ident[0:E, 0:E])
                mm.then_inc(lg_ready, 1)

            def batch(b, first=False, last=False):
                for h in range(H):
                    if h + AHEAD < H:
                        scores(b, h + AHEAD)
                    elif not last:
                        scores(b + 1, h + AHEAD - H)
                    if h == C_AT and not last:
                        pe.wait_ge(q_read, G * (b + 1))
                        latents(b + 1)
                    if h == KR_AT and not last:
                        pe.wait_ge(v_done, 2 * b + 2)
                        rotary_keys(b + 1, 0)
                    if h == FLIP_AT and not first:
                        if last:
                            pe.wait_ge(gt_done, 2 * DC)
                        else:
                            pe.wait_ge(clo_done, 2 * b + 4)
                            pe.wait_ge(kr_steps, 3 * b + 4)
                        flip(b - 1)
                    if h == KRB_AT and not last:
                        rotary_keys(b + 1, 1)
                    if not last:
                        if h in QA_AT:
                            if QA_AT[h] == 0:
                                pe.wait_ge(c_stacked, 32 * (b + 2))
                                if first:
                                    pe.wait_ge(kr_steps, 3 * b + 4)
                                else:
                                    pe.wait_ge(on_done, DC * b)
                            queries(b + 1, QA_AT[h])
                        if h in QB_AT:
                            partners(b + 1, QB_AT[h])
                        if h in KK_AT:
                            if KK_AT[h] == 0:
                                pe.wait_ge(kr_steps, 3 * b + 5)
                            keys(b + 1, KK_AT[h])
                    if last:
                        if h in BACK_AT:
                            turn_back(BACK_AT[h])
                        if h in TURN_AT:
                            turn_rows(TURN_AT[h])
                        if h in GATE_AT:
                            gate(GATE_AT[h])
                    if h in O_AT and not first:
                        if last:
                            pe.wait_ge(lg_done, GATED)
                        elif O_AT[h] == 0:
                            pe.wait_ge(q_read, G * (b + 2))
                            pe.wait_ge(k_read, G * (b + 2))
                        output(b - 1, O_AT[h])
                    if h == V_AT and not last:
                        pe.wait_ge(partners_read, G * (b + 2))
                        if first:
                            pe.wait_ge(k_read, G * (b + 2))
                        else:
                            pe.wait_ge(res_done, KB * b)
                        values(b + 1)
                    weigh(b, h, first)
                    if h % HG == 0 and h:
                        turn(b, h // HG - 1)
                    elif h == 0 and not first:
                        turn(b - 1, G - 1)

            pe.wait_ge(down_in, 32)
            latents(0)
            for part in range(2):
                rotary_keys(0, part)
            pe.wait_ge(kr_steps, 2)
            pe.wait_ge(wlo_done, 3)
            pe.wait_ge(consts_in, 16 * CONSTS)
            pe.wait_ge(ones_set, 1)
            values(0)
            pe.wait_ge(v_done, 2)
            for g in range(2):
                queries(0, g)
                partners(0, g)
                keys(0, g)
            for h in range(AHEAD):
                scores(0, h, first=h == 0)
            for g in range(2, G):
                queries(0, g)
                partners(0, g)
                keys(0, g)
            batch(0, first=True)
            with pe.Fori(1, B - 1) as b:
                batch(b)
            batch(B - 1, last=True)
            turn(B - 1, G - 1)
            flip(B - 1)
            for half in range(2):
                output(B - 1, half)

        @block.scalar
        def _(act):
            def latents(b):
                act.wait_ge(c_ready, b + 1)
                act.activation(c2[0:LAT, 0, :], ps[0:LAT, PROJ, :], ACT.Copy).then_inc(chi_done, 1)
                act.activation(c2[LAT:P, 1, :], ps[LAT:P, PROJ, :], ACT.Copy).then_inc(chi_done, 1)

            def stack_latents(b):
                act.wait_ge(clo_done, 2 * b + 2)
                act.dma_start(c2[LAT:P, 0, :].bitcast(F32), clo[0:LAT, :].bitcast(F32)).then_inc(c_stacked, 16)
                act.dma_start(c2[0:LAT, 1, :].bitcast(F32), clo[LAT:P, :].bitcast(F32)).then_inc(c_stacked, 16)

            def values(b, first=False):
                for n in range(2):
                    if n == 0 and not first:
                        act.wait_ge(v_placed, G * b)
                    act.wait_ge(v_ready, 2 * b + n + 1)
                    act.activation(vnext[:, 2 * n:2 * n + 2, :, :],
                                   ps[:, PROJ + 1 + n, :].rearrange("p (t h d) -> p t h d", t=2, h=H),
                                   ACT.Copy).then_inc(v_done, 1)

            def place_values(b, g, first=False):
                if not first:
                    act.wait_ge(pv_done, H * (b - 1) + HG * (g + 1))
                act.wait_ge(v_done, 2 * b + 2)
                act.activation(v[:, :, HG * g:HG * (g + 1), 0:DH],
                               vnext[:, :, HG * g:HG * (g + 1), :], ACT.Copy).then_inc(v_placed, 1)

            def high_parts(b, g, first=False):
                n = G * b + g
                if g % 2 == 0 and not first:
                    for i in range(HG):
                        act.wait_ge(stacked[i], STACK * (2 * b + g // 2))
                act.wait_ge(q_done, n + 1)
                act.activation(qhi[:, g % 2, :], qt[:, g % 2, :], ACT.Copy).then_inc(hi_done, 1)
                act.wait_ge(k_read, n + 1)
                act.activation(khi[:, g % 2, :], kt[:, g % 2, :], ACT.Copy).then_inc(hi_done, 1)

            def exps(b, h, first=False):
                act.wait_ge(s01_ready, H * b + h + 1)
                if not (first and h < 4):
                    act.wait_ge(pv_done, H * b + h - 3)
                act.activation(e[:, h % 4, 0:AT[2] - P], ps[:, SC:SC + 2, :].rearrange("p a s -> p (a s)")[:, 0:AT[2] - P],
                               ACT.Exp, scale=SCALE).then_inc(exp01_done, 1)
                act.wait_ge(s_ready, H * b + h + 1)
                act.activation(e[:, h % 4, AT[2] - P:EW], ps[:, SC + 2, P:], ACT.Exp, scale=SCALE).then_inc(exp_done, 1)

            def outputs(b, g, first=False):
                act.wait_ge(pv_done, H * b + HG * (g + 1))
                if not (first and g < 2):
                    act.wait_ge(turned, G * b + g - 1)
                act.activation(ot[:, g % 2, :], ps[:, PV + g % 2, :], ACT.Copy).then_inc(ot_done, 1)

            def flips(b):
                for c in range(DC):
                    act.wait_ge(flipped, DC * b + c + 1)
                    act.activation(on[:, c, :], ps[:, PROJ + c, :], ACT.Copy).then_inc(on_done, 1)

            def turned_row(q):
                if q < 2:
                    act.wait_ge(lo_done, 2 * G * B)
                else:
                    act.wait_ge(lt_ready, q - 1)
                for k in range(DC):
                    act.wait_ge(gt_ready, DC * q + k + 1)
                    act.activation(turned_rows[q % 2][:, k, :], ps[:, PROJ + k, :], ACT.Copy).then_inc(gt_done, 1)

            def gated(q):
                act.wait_ge(lt_ready, q + 1)
                if q >= 2:
                    act.wait_ge(lg_ready, q - 1)
                act.activation(lt[0:E, q % 2, :], ps[0:E, PROJ + 2, :], ACT.Copy).then_inc(lt_done, 1)

            def batch(b, first=False, last=False):
                for h in range(H):
                    if h + AHEAD < H:
                        exps(b, h + AHEAD, first)
                    elif not last:
                        exps(b + 1, h + AHEAD - H)
                    if h % HG == 0 and h:
                        outputs(b, h // HG - 1, first)
                    elif h == 0 and not first:
                        outputs(b - 1, G - 1)
                    if h in PLACE_AT:
                        place_values(b, PLACE_AT[h], first)
                    if h == C_AT and not last:
                        latents(b + 1)
                    if h == C_AT + 1 and not last:
                        stack_latents(b + 1)
                    if h == FLIP_AT and not first:
                        flips(b - 1)
                    if last and h in TURN_AT:
                        turned_row(TURN_AT[h])
                    if last and h in GATE_AT:
                        gated(GATE_AT[h])
                    if h in HIGH_AT and not last:
                        for g in HIGH_AT[h]:
                            high_parts(b + 1, g)
                    if h == V_AT and not last:
                        values(b + 1)
                        place_values(b + 1, 0)

            latents(0)
            act.wait_ge(consts_in, 16 * CONSTS)
            act.activation(wkv2[:, :], e[:, 1, 0:KW], ACT.Copy).then_inc(whi_done, 1)
            act.activation(wq2[:, :], e[:, 0, 0:QW], ACT.Copy).then_inc(whi_done, 1)
            stack_latents(0)
            values(0, first=True)
            place_values(0, 0, first=True)
            for g in range(2):
                high_parts(0, g, first=True)
            act.wait_ge(wlo_done, 3)
            for h in range(AHEAD):
                exps(0, h, first=True)
            for g in range(2, G):
                high_parts(0, g)
            batch(0, first=True)
            with act.Fori(1, B - 1) as b:
                batch(b)
            batch(B - 1, last=True)
            outputs(B - 1, G - 1)
            flips(B - 1)

        @block.gpsimd
        def _(pool):
            def rotate(b, g):
                n = G * b + g
                pool.wait_ge(partners_read, n + 1)
                pool.tensor_tensor(qt[:, g % 2, :], qt[:, g % 2, :], sinpart[:, g % 2, :], ALU.add).then_inc(q_done, 1)

            def mask(b, h):
                pool.wait_ge(clip_done, H * b + h + 1)
                a = e[:, h % 4, 0:2 * S].rearrange("p (a s) -> p a s", a=2)[:, :, 0:P]
                c = e[:, h % 4, AT[3]:AT[2] + P].rearrange("p (a s) -> p a s", a=2)
                seen = causal[:, :, :].to_broadcast([P, 2, P])
                pool.tensor_tensor(a, a, seen, ALU.mult)
                pool.tensor_tensor(c, c, seen, ALU.mult).then_inc(mask_done, 1)

            def deviations(b):
                pool.wait_ge(var_done, b + 1)
                pool.tensor_tensor(rstd[:, :], var[:, :], minus_half[:, :], ALU.pow).then_inc(rstd_done, 1)

            def batch(b, first=False, last=False):
                for h in range(H):
                    if h + AHEAD < H:
                        mask(b, h + AHEAD)
                    elif not last:
                        mask(b + 1, h + AHEAD - H)
                    if h in QB_AT and not last:
                        rotate(b + 1, QB_AT[h])
                    if O_AT.get(h) == 1 and not first:
                        deviations(b - 1)

            pool.memset(v[:, :, :, DH:], 1.0).then_inc(ones_set, 1)
            pool.memset(minus_half[:, :], -0.5)
            pool.wait_ge(consts_in, 16 * CONSTS)
            for g in range(2):
                rotate(0, g)
            for h in range(AHEAD):
                mask(0, h)
            for g in range(2, G):
                rotate(0, g)
            batch(0, first=True)
            with pool.Fori(1, B - 1) as b:
                batch(b)
            pool.wait_ge(kr_ready, 2 * B)
            pool.memset(zeros, 0.0).then_inc(zeros_set, 1)
            batch(B - 1, last=True)
            deviations(B - 1)

        @block.vector
        def _(dve):
            low, high = float(np.exp(-CLIP * SCALE)), float(np.exp(CLIP * SCALE))

            def latents(b, first=False):
                if not first:
                    dve.wait_ge(c_stacked, 32 * b)
                for n, half in enumerate((slice(0, LAT), slice(LAT, P))):
                    dve.wait_ge(chi_done, 2 * b + n + 1)
                    dve.tensor_tensor(clo[half, :], ps[half, PROJ, :], c2[half, n, :].bitcast(F32),
                                      ALU.subtract).then_inc(clo_done, 1)

            def rotary_keys(b, first=False):
                if not first:
                    dve.wait_ge(k_read, G * b)
                dve.wait_ge(kr_ready, 2 * b + 1)
                dve.tensor_tensor(kr[:, :], ps[:, PROJ + 1, :], cs[:, 0, :], ALU.mult).then_inc(kr_steps, 1)

            def rotary_keys_partners(b, first=False):
                if not first:
                    dve.wait_ge(q_done, G * b)
                dve.wait_ge(kr_ready, 2 * b + 2)
                dve.tensor_tensor(krsin, ps[:, PROJ + 2, :], cs[:, 1, :], ALU.mult).then_inc(kr_steps, 1)
                dve.wait_ge(kr_steps, 3 * b + 2)
                dve.tensor_tensor(kr[:, :], kr[:, :], krsin, ALU.add).then_inc(kr_steps, 1)

            def queries(b, g, first=False):
                n = G * b + g
                if not (first and g < 2):
                    dve.wait_ge(lo_done, 2 * n - 2)
                dve.wait_ge(q_ready, 2 * n + 1)
                dve.tensor_tensor(qt[:, g % 2, :], ps[:, PROJ, :], cs[:, 0, :], ALU.mult).then_inc(q_read, 1)

            def partners(b, g):
                dve.wait_ge(q_ready, 2 * (G * b + g) + 2)
                dve.tensor_tensor(sinpart[:, g % 2, :], ps[:, PROJ + 1, :], cs[:, 1, :], ALU.mult).then_inc(partners_read, 1)

            def keys(b, g):
                if g == 0:
                    dve.wait_ge(kr_steps, 3 * b + 3)
                dve.wait_ge(k_ready, G * b + g + 1)
                dve.tensor_tensor(kt[:, g % 2, :], ps[:, PROJ + 2, :], kr[:, :], ALU.add).then_inc(k_read, 1)

            def low_parts(b, g, first=False):
                n = G * b + g
                if g % 2 == 0 and not first:
                    for i in range(HG):
                        dve.wait_ge(stacked[i], STACK * (2 * b + g // 2))
                for part, lo, full, hi in ((1, qlo, qt, qhi), (2, klo, kt, khi)):
                    dve.wait_ge(hi_done, 2 * n + part)
                    dve.tensor_tensor(lo[:, g % 2, :], full[:, g % 2, :], hi[:, g % 2, :].bitcast(F32),
                                      ALU.subtract).then_inc(lo_done, 1)

            def clip(b, h):
                dve.wait_ge(exp_done, H * b + h + 1)
                dve.tensor_scalar(e[:, h % 4, :], e[:, h % 4, :], high, low, ALU.min, ALU.max).then_inc(clip_done, 1)

            def normalise(b, g, first=False):
                n = G * b + g
                if g == 0 and not first:
                    dve.wait_ge(flipped, DC * b)
                dve.wait_ge(turned, n + 1)
                both = ps[:, PV + g % 2, 0:KB * PICKED].rearrange("p (t w) -> p t w", t=KB)
                dve.reciprocal(rec[:, g % 2, :, :], both[:, :, HG * DH:]).then_inc(rec_done, 1)
                dve.wait_ge(rec_done, n + 1)
                dve.tensor_tensor(onq[:, :, g * HG * DH:(g + 1) * HG * DH].rearrange("p t (i d) -> p t i d", i=HG),
                                  both[:, :, 0:HG * DH].rearrange("p t (i d) -> p t i d", i=HG),
                                  rec[:, g % 2, :, :].unsqueeze(3).to_broadcast([P, KB, HG, DH]),
                                  ALU.mult).then_inc(normed, 1)

            def residual(b, half):
                if half == 0:
                    dve.wait_ge(rows_in, 16 * (b + 1))
                dve.wait_ge(a_ready, 2 * b + half + 1)
                bank = PROJ + (0 if half else 2)
                for t in range(2 * half, 2 * half + 2):
                    dve.tensor_tensor(row[:, t, :], ps[:, bank, (t % 2) * D:(t % 2) * D + D],
                                      res[:, bass.ds(b * KB + t, 1), :].rearrange("p a d -> p (a d)"),
                                      ALU.add).then_inc(res_done, 1)
                    dve.wait_ge(res_done, KB * b + t + 1)
                    dve.bn_stats(bn[:, t, :], row[:, t, :]).then_inc(bn_done, 1)

            def variance(b):
                dve.wait_ge(consts_in, 16 * CONSTS)
                dve.wait_ge(bn_done, KB * b + KB)
                for t in range(KB):
                    dve.bn_aggr(mv[:, t, :], bn[:, t, :]).then_inc(mv_done, 1)
                dve.wait_ge(mv_done, KB * (b + 1))
                dve.tensor_scalar(var[:, :], mv[:, :, 1], EPS, None, ALU.add).then_inc(var_done, 1)

            def layernorm(b):
                dve.wait_ge(rstd_done, b + 1)
                for t in range(KB):
                    ins = dve.tensor_scalar(res[:, bass.ds(b * KB + t, 1), :].rearrange("p a d -> p (a d)"), row[:, t, :],
                                            mv[:, t, 0:1], rstd[:, t:t + 1], ALU.subtract, ALU.mult)
                ins.then_inc(rows_done, 1)

            def logits_of(q):
                dve.wait_ge(lg_ready, q + 1)
                dve.tensor_tensor(logits[:, KB * q:KB * (q + 1), :],
                                  ps[:, PROJ + 2, 0:KB * E].rearrange("p (t e) -> p t e", t=KB),
                                  gb[:, :].unsqueeze(1).to_broadcast([P, KB, E]), ALU.add).then_inc(lg_done, 1)

            def batch(b, first=False, last=False):
                for h in range(H):
                    if h + AHEAD < H:
                        clip(b, h + AHEAD)
                    elif not last:
                        clip(b + 1, h + AHEAD - H)
                    if h % HG == 1 and h > HG:
                        normalise(b, h // HG - 1, first)
                    elif h == 1 and not first:
                        normalise(b - 1, G - 1)
                    if h == C_AT and not last:
                        latents(b + 1)
                    if h == KR_AT and not last:
                        rotary_keys(b + 1)
                    if h == KRB_AT and not last:
                        rotary_keys_partners(b + 1)
                    if not last:
                        if h in QA_AT:
                            queries(b + 1, QA_AT[h])
                        if h in QB_AT:
                            partners(b + 1, QB_AT[h])
                        if h in KK_AT:
                            keys(b + 1, KK_AT[h])
                        if h in LOW_AT:
                            for g in LOW_AT[h]:
                                low_parts(b + 1, g)
                    if last and h in BACK_AT:
                        logits_of(BACK_AT[h])
                    if h in O_AT and not first:
                        residual(b - 1, O_AT[h])
                        if O_AT[h] == 1:
                            variance(b - 1)
                    if h == V_AT and not first:
                        layernorm(b - 1)

            dve.wait_ge(consts_in, 16 * CONSTS)
            latents(0, first=True)
            rotary_keys(0, first=True)
            rotary_keys_partners(0, first=True)
            dve.wait_ge(whi_done, 2)
            dve.tensor_tensor(wlo[LAT:P, 0:KW], e[LAT:P, 1, 0:KW], wkv2[LAT:P, :].bitcast(F32), ALU.subtract).then_inc(wlo_done, 1)
            dve.tensor_tensor(wlo[0:LAT, :], e[0:LAT, 0, 0:QW], wq2[0:LAT, :].bitcast(F32), ALU.subtract).then_inc(wlo_done, 2)
            for g in range(2):
                queries(0, g, first=True)
                partners(0, g)
                keys(0, g)
                low_parts(0, g, first=True)
            for h in range(AHEAD):
                clip(0, h)
            for g in range(2, G):
                queries(0, g)
                partners(0, g)
                keys(0, g)
                low_parts(0, g)
            batch(0, first=True)
            with dve.Fori(1, B - 1) as b:
                batch(b)
            batch(B - 1, last=True)
            normalise(B - 1, G - 1)
            for half in range(2):
                residual(B - 1, half)
            variance(B - 1)
            layernorm(B - 1)


def experts(nc, res, ident, gw, gb, logits, slots_in, slots_out, w1, w2, b1, b2, masks, numbers, out):
    C = TS // P
    HC = HID // P
    HEAD = 4
    LAST = HEAD + TILES
    END = T // TS + TILES
    PIECE = DC * HID // HC * 2
    HALF = HC // 2
    RANKS = 4
    with ExitStack() as ctx:
        def sb(name, shape, dt=F32):
            return ctx.enter_context(nc.sbuf_tensor(name, shape, dt))

        def sem(name):
            return ctx.enter_context(nc.semaphore(name))

        w1raw, w2raw = sb("w1raw", [P, DC, HID]), sb("w2raw", [P, HC, D])
        w1hi, w1lo = sb("w1hi", [P, 2, DC, HID], F32R), sb("w1lo", [P, 2, DC, HID], F32R)
        w2hi, w2lo = sb("w2hi", [P, 2, HC, D], F32R), sb("w2lo", [P, 2, HC, D], F32R)
        bias1, bias2 = sb("bias1", [P, 2, HC]), sb("bias2", [P, 2, D])
        rows = sb("rows", [P, 2, C, D])
        xhi, xlo = sb("xhi", [P, 2, DC, TS], F32R), sb("xlo", [P, 2, DC, TS], F32R)
        yT = sb("yT", [P, 2, DC, TS])
        lt = sb("lt", [E, 2, TS])
        h = sb("h", [P, 2, TS])
        hhi, hlo = sb("hhi", [P, 2, TS], F32R), sb("hlo", [P, 2, TS], F32R)
        ys = sb("ys", [P, 2, C, D])
        before, ones = sb("before", [P, P]), sb("ones", [P, P])
        nums = sb("nums", [P, E + TILES])
        first, second, both = sb("first", [P, NT, E]), sb("second", [P, NT, E]), sb("both", [P, NT, E])
        work = sb("work", [P, NT, E])
        total, upto, zero = sb("total", [P, E, NT]), sb("upto", [P, E, NT]), sb("zero", [P, E * NT])
        best, pick, next_best = sb("best", [P, NT]), sb("pick", [P, NT]), sb("next_best", [P, NT])
        gap, den = sb("gap", [P, NT]), sb("den", [P, NT])
        wt = sb("wt", [P, TOP, NT])
        slotf, slot = sb("slotf", [P, TOP, NT]), sb("slot", [P, TOP, NT], I32)
        count, tiles_i, tiles_f = sb("count", [P, E]), sb("tiles_i", [P, E], I32), sb("tiles_f", [P, E])
        tiles_upto, base = sb("tiles_upto", [P, E]), sb("base", [P, E])
        passed, owner, owner_i = sb("passed", [P, TILES, E]), sb("owner", [P, TILES]), sb("owner_i", [P, TILES], I32)
        back = sb("back", [P, 4, TOP, D])
        bn, mv = sb("bn2", [P, 2, 6]), sb("mv2", [P, 2, 2])
        var, rstd, minus_half = sb("var2", [P, 2]), sb("rstd2", [P, 2]), sb("minus_half2", [P, 1])
        fin = sb("fin", [P, 4, D])
        ps = ctx.enter_context(nc.psum_tensor("ps2", [P, 8, 512], F32))

        consts_in, minus_set = sem("consts_in2"), sem("minus_set")
        gt_ready, gt_done, lg_ready, lg_done = sem("gt_ready"), sem("gt_done"), sem("lg_ready"), sem("lg_done")
        lt_ready, lt_done = sem("lt_ready"), sem("lt_done")
        last_hhi_done, first_w1_lo = sem("last_hhi_done"), sem("first_w1_lo")
        route_step, gap_done, gap_exp, both_done, ranks_ready, slots_known = (
            sem("route_step"), sem("gap_done"), sem("gap_exp"), sem("both_done"), sem("ranks_ready"), sem("slots_known"))
        sent = [sem(f"sent{n}") for n in range(2)]
        GROUP = 16 * TOP * C
        w1_in, w2_in, b_in, x_in = sem("w1_in"), sem("w2_in"), sem("b_in"), sem("x_in2")
        w_hi, w_lo = sem("w_hi"), sem("w_lo")
        tr_ready, xhi_done, xlo_done = sem("tr_ready"), sem("xhi_done"), sem("xlo_done")
        m1_ready, gelu_done, hhi_done, h_done = sem("m1_ready"), sem("gelu_done"), sem("hhi_done"), sem("h_done")
        y_ready, ysum, y_done, y_out = sem("y_ready"), sem("ysum"), sem("y_done"), sem("y_out")
        back_in = [sem(f"back_in{n}") for n in range(4)]
        c_step, var_done, rstd_done, fin_done = sem("c_step"), sem("var_done2"), sem("rstd_done2"), sem("fin_done")
        fin_out = [sem(f"fin_out{n}") for n in range(4)]

        block = ctx.enter_context(nc.Block())
        CONSTS = 3
        Q = NT // C - GATED

        def slots_tile(dram, at):
            return dram.rearrange("s d -> (s d)")[bass.ds(at, TS * D)].rearrange("(p c d) -> p c d", p=P, c=C)


        def is_shared(s):
            return s < HEAD or s >= LAST

        def act_halves(s):
            return isinstance(s, int) and s >= LAST

        def tokens(s):
            n = (s if s < HEAD else s - TILES) * C
            return range(n, n + C)

        LAG = 4
        LASTS = END - LAST

        @block.sync
        def _(sp):
            def load_w1(src):
                sp.dma_start(w1raw[:, :, :], src).then_inc(w1_in, 16)

            def load_w2(src):
                sp.dma_start(w2raw[:, :, :], src).then_inc(w2_in, 16)

            def load_b(e, u):
                sp.dma_start(bias1[:, u, :], b1[bass.ds(e, 1)].rearrange("e p c -> p (e c)")).then_inc(b_in, 16)
                sp.dma_start(bias2[:, u, :], b2[bass.ds(e, 1), :].to_broadcast([P, D])).then_inc(b_in, 16)

            def w1_of(e):
                return w1[bass.ds(e, 1)].rearrange("e (k p) n -> p (e k) n", p=P)

            def w2_of(e):
                return w2[bass.ds(e, 1)].rearrange("e (c p) n -> p (e c) n", p=P)

            for dst, src in ((before, masks[:, 2, :]), (ones, masks[:, 3, :]),
                             (nums, numbers)):
                sp.dma_start(dst[:], src).then_inc(consts_in, 16)
            load_w1(w1_of(E))
            load_w2(w2_of(E))
            load_b(E, 1)

            def prefetch(s, u, shared_next=False):
                r = s + 1 - HEAD
                at = r * TS * D if isinstance(r, int) else sp.snap(r * (TS * D))
                e = E if shared_next else sp.value_load(owner_i[0:1, bass.ds(r, 1)], min_val=0, max_val=E - 1)
                sp.wait_ge(w_lo, HC * r + HALF)
                load_w1(w1_of(e))
                if not shared_next:
                    sp.wait_ge(x_in, 16 * r)
                    sp.wait_ge(tr_ready, 2 * s)
                    sp.dma_start(rows[:, 1 - u, :, :], slots_tile(slots_in, at)).then_inc(x_in, 16)
                sp.wait_ge(w_lo, HC * r + HC)
                load_w2(w2_of(e))
                sp.wait_ge(y_done, s)
                sp.wait_ge(b_in, 32 * (r + 1))
                load_b(e, 1 - u)
                return r

            def store(s, u):
                r = s - HEAD
                at = r * TS * D if isinstance(r, int) else sp.snap(r * (TS * D))
                sp.wait_ge(y_out, 16 * r + 32)
                sp.wait_ge(y_done, s + 1)
                sp.dma_start(slots_tile(slots_out, at), ys[:, u, :, :]).then_inc(y_out, 16)

            sp.sem_inc(y_out, 32)
            sp.wait_ge(slots_known, 1)
            e = sp.value_load(owner_i[0:1, 0:1], min_val=0, max_val=E - 1)
            sp.wait_ge(w_lo, HALF)
            load_w1(w1_of(e))
            sp.wait_ge(w_lo, HC)
            load_w2(w2_of(e))
            sp.wait_ge(b_in, 32)
            load_b(e, 0)
            for n in range(2):
                sp.wait_ge(sent[n], GROUP * NT // C // 2)
            sp.dma_start(rows[:, 0, :, :], slots_tile(slots_in, 0)).then_inc(x_in, 16)
            prefetch(HEAD, 0)
            with sp.Fori(0, (TILES - 3) // 2) as i:
                for u in (1, 0):
                    s = HEAD + 2 * i + (1 if u else 2)
                    prefetch(s, u)
                    store(s - 1, 1 - u)
            prefetch(LAST - 2, 1)
            store(LAST - 3, 0)
            prefetch(LAST - 1, 0, shared_next=True)
            store(LAST - 2, 1)
            store(LAST - 1, 0)
            for t in range(NT):
                sp.wait_ge(fin_done, t + 1)
                sp.dma_start(out[t * P:(t + 1) * P, :], fin[:, t % 4, :]).then_inc(fin_out[t % 4], 16)
            for n in range(4):
                sp.wait_ge(fin_out[n], 16 * NT // 4)

        @block.tensor
        def _(pe):
            for q in range(Q + 2):
                if q < Q:
                    u = q % 2
                    if q >= 2:
                        pe.wait_ge(gt_done, 2 * (q - 1))
                    for k in range(DC):
                        for c in range(C):
                            mm = pe.transpose(ps[:, 2 * u + k, c * P:(c + 1) * P],
                                              res[:, C * (GATED + q) + c, k * P:(k + 1) * P], ident[:, :])
                        mm.then_inc(gt_ready, 1)
                if 1 <= q <= Q:
                    u = (q - 1) % 2
                    pe.wait_ge(gt_done, 2 * q)
                    if q >= 3:
                        pe.wait_ge(lt_done, q - 2)
                    for k in range(DC):
                        mm = pe.matmul(ps[0:E, 4 + u, :], gw[:, k, :], yT[:, u, k, :], start=k == 0, stop=k == DC - 1)
                    mm.then_inc(lt_ready, 1)
                if q >= 2:
                    u = q % 2
                    pe.wait_ge(lt_done, q - 1)
                    if q >= 4:
                        pe.wait_ge(lg_done, q - 3)
                    for c in range(C):
                        mm = pe.transpose(ps[:, 6 + u, c * E:(c + 1) * E], lt[:, u, c * P:(c + 1) * P], ident[0:E, 0:E])
                    mm.then_inc(lg_ready, 1)

            def ranks():
                pe.wait_ge(both_done, 1)
                pe.matmul(ps[:, RANKS, 0:NT * E], before[:, :], both[:, :, :].rearrange("p t e -> p (t e)"),
                          start=True, stop=True)
                pe.matmul(ps[:, RANKS, NT * E:2 * NT * E], ones[:, :], both[:, :, :].rearrange("p t e -> p (t e)"),
                          start=True, stop=True).then_inc(ranks_ready, 1)

            def turn(s, u):
                if not is_shared_now:
                    pe.wait_ge(x_in, 16 * (s - HEAD + 1))
                for k in range(DC):
                    for c in range(C):
                        src = res[:, tokens(s)[c], :] if is_shared_now else rows[:, u, c, :]
                        mm = pe.transpose(ps[:, 6 + k, c * P:(c + 1) * P], src[:, k * P:(k + 1) * P], ident[:, :])
                    mm.then_inc(tr_ready, 1)

            def up(s, u, w, c, load=None):
                if c == 0:
                    pe.wait_ge(xhi_done, 2 * s + 2)
                    pe.wait_ge(xlo_done, 2 * s + 2)
                    if load is not None:
                        pe.wait_ge(w_lo, HC * load + HALF)
                cols = slice(c * P, (c + 1) * P)
                n = 0
                for k in range(DC):
                    for a, b in ((w1hi, xhi), (w1hi, xlo), (w1lo, xhi)):
                        mm = pe.matmul(ps[:, c % 2, :], a[:, w, k, cols], b[:, u, k, :], start=n == 0, stop=n == 3 * DC - 1)
                        n += 1
                mm.then_inc(m1_ready, 1)

            def down(s, u, w, c, load=None):
                if c == 0 and load is not None:
                    pe.wait_ge(w_lo, HC * load + HC)
                pe.wait_ge(h_done, HC * s + c + 1)
                for q in range(C):
                    to = ps[:, 2 + 2 * u + q // 2, (q % 2) * D:(q % 2) * D + D]
                    for n, (a, b) in enumerate(((hhi, w2hi), (hhi, w2lo), (hlo, w2hi))):
                        mm = pe.matmul(to, a[:, c % 2, q * P:(q + 1) * P], b[:, w, c, :],
                                       start=c == 0 and n == 0 and q % 2 == 0, stop=c == HC - 1 and n == 2,
                                       skip_group_check=True)
                if c == HC - 1:
                    mm.then_inc(y_ready, 1)

            def tile(s, u, w, load, nxt):
                nonlocal is_shared_now
                for c in range(HC):
                    if c < HC - 1:
                        up(s, u, w, c + 1)
                    elif nxt:
                        up(s + 1, nxt[0], nxt[1], 0, nxt[2])
                    down(s, u, w, c, load)
                    if c == 3 and nxt:
                        is_shared_now = nxt[3]
                        turn(s + 1, nxt[0])

            is_shared_now = True
            pe.wait_ge(lg_done, Q)
            turn(0, 0)
            pe.wait_ge(consts_in, 16 * CONSTS)
            pe.wait_ge(lt_done, Q)
            ranks()
            up(0, 0, 1, 0, 0)
            for s in range(HEAD):
                tile(s, s % 2, 1, 0, ((s + 1) % 2, 1, 0, True) if s < HEAD - 1 else (0, 0, 1, False))
            with pe.Fori(0, (TILES - 1) // 2) as i:
                for u in range(2):
                    s, load = HEAD + 2 * i + u, 2 * i + u + 1
                    tile(s, u, u, load, (1 - u, 1 - u, load + 1, False))
            tile(LAST - 1, 0, 0, TILES, (1, 1, TILES + 1, True))
            for s in range(LAST, END):
                tile(s, s % 2, 1, TILES + 1, ((s + 1) % 2, 1, TILES + 1, True) if s < END - 1 else None)

        def split(eng, load, w, c, lo, done=w_lo):
            if c < HALF:
                k, cols = c // 2, slice((c % 2) * 512, (c % 2) * 512 + 512)
                raw, hi, low = w1raw[:, k, cols], w1hi[:, w, k, cols], w1lo[:, w, k, cols]
            else:
                n = 2 * (c - HALF)
                raw, hi, low = w2raw[:, n:n + 2, :], w2hi[:, w, n:n + 2, :], w2lo[:, w, n:n + 2, :]
            if lo:
                eng.wait_ge(w_hi, HC * load + c + 1)
                eng.tensor_tensor(low, raw, hi.bitcast(F32), ALU.subtract).then_inc(done, 1)
            else:
                if c == 0:
                    eng.wait_ge(w1_in, 16 * (load + 1))
                if c == HALF:
                    eng.wait_ge(w2_in, 16 * (load + 1))
                eng.activation(hi, raw, ACT.Copy).then_inc(w_hi, 1)

        @block.scalar
        def _(act):
            for q in range(Q + 1):
                if q < Q:
                    act.wait_ge(gt_ready, 2 * q + 2)
                    if q >= 2:
                        act.wait_ge(lt_ready, q - 1)
                    act.activation(yT[:, q % 2, 0, :], ps[:, 2 * (q % 2), :], ACT.Copy).then_inc(gt_done, 1)
                    act.activation(yT[:, q % 2, 1, :], ps[:, 2 * (q % 2) + 1, :], ACT.Copy).then_inc(gt_done, 1)
                if q >= 1:
                    act.wait_ge(lt_ready, q)
                    if q >= 3:
                        act.wait_ge(lg_ready, q - 2)
                    act.activation(lt[:, (q - 1) % 2, :], ps[0:E, 4 + (q - 1) % 2, :], ACT.Copy).then_inc(lt_done, 1)
            for c in range(HC):
                split(act, 0, 1, c, False)

            def turned(s, u):
                for k in range(DC):
                    act.wait_ge(tr_ready, 2 * s + k + 1)
                    act.activation(xhi[:, u, k, :], ps[:, 6 + k, :], ACT.Copy).then_inc(xhi_done, 1)

            def tile(s, u, w, nxt=None, load=None, routing=False):
                for c in range(HC):
                    act.wait_ge(m1_ready, HC * s + c + 1)
                    if c == 0:
                        act.wait_ge(b_in, 32 * bias_loads)
                    act.activation(h[:, c % 2, :], ps[:, c % 2, :], ACT.Gelu, bias=bias1[:, w, c:c + 1]).then_inc(gelu_done, 1)
                    if act_halves(s):
                        act.wait_ge(gelu_done, HC * s + c + 1)
                        act.activation(hhi[:, c % 2, :], h[:, c % 2, :], ACT.Copy).then_inc(last_hhi_done, 1)
                    if c == 4 and nxt:
                        turned(s + 1, 1 - u)
                    if c == 4 and routing:
                        act.wait_ge(gap_done, 1)
                        act.activation(gap[:, :], gap[:, :], ACT.Exp).then_inc(gap_exp, 1)
                    if load is not None:
                        if c == 0:
                            act.wait_ge(y_ready, s)
                        split(act, load[0], load[1], c, False)

            turned(0, 0)
            for s in range(HEAD):
                bias_loads = 1
                tile(s, s % 2, 1, True, (1, 0) if s == HEAD - 1 else None, routing=s == 0)
            with act.Fori(0, (TILES - 1) // 2) as i:
                for u in range(2):
                    bias_loads = 2 * i + u + 2
                    tile(HEAD + 2 * i + u, u, u, True, (2 * i + u + 2, 1 - u))
            bias_loads = TILES + 1
            tile(LAST - 1, 0, 0, True, (TILES + 1, 1))
            bias_loads = TILES + 2
            for s in range(LAST, END):
                tile(s, s % 2, 1, s < END - 1)

        @block.gpsimd
        def _(pool):
            pool.memset(minus_half[:, :], -0.5).then_inc(minus_set, 1)
            pool.wait_ge(minus_set, 1)
            for c in range(HALF):
                split(pool, 0, 1, c, True, first_w1_lo)
            pool.wait_ge(slots_known, 1)
            for t in range(NT):
                for n in range(TOP):
                    pool.indirect_dma_start(slots_in, bass.IndirectOffsetOnAxis(ap=slot[:, n, t:t + 1], axis=0),
                                            res[:, t, :], None).then_inc(sent[t // C % 2], 16)
                if t % C == C - 1 and t >= C:
                    pool.wait_ge(sent[(t // C - 1) % 2], GROUP * ((t // C - 1) // 2 + 1))

            def fetch(t):
                if t >= 4:
                    pool.wait_ge(c_step, 4 * (t - 4) + 2)
                for n in range(TOP):
                    pool.indirect_dma_start(back[:, t % 4, n, :], None, slots_out,
                                            bass.IndirectOffsetOnAxis(ap=slot[:, n, t:t + 1], axis=0)).then_inc(back_in[t % 4], 16)

            def root(t):
                pool.wait_ge(var_done, t + 1)
                pool.tensor_tensor(rstd[:, t % 2:t % 2 + 1], var[:, t % 2:t % 2 + 1], minus_half[:, :], ALU.pow).then_inc(rstd_done, 1)

            pool.wait_ge(y_out, 16 * TILES + 32)
            for t in range(NT + 4):
                if t < NT:
                    fetch(t)
                if t >= 4:
                    root(t - 4)

        @block.vector
        def _(dve):
            steps = 0

            def step(ins):
                nonlocal steps
                ins.then_inc(route_step, 1)
                steps += 1
                dve.wait_ge(route_step, steps)

            def over(ap, n):
                return ap.unsqueeze(2).to_broadcast([P, ap.shape[1], n])

            def across(ap, n):
                return ap.unsqueeze(1).to_broadcast([P, n, ap.shape[1]])

            for q in range(Q):
                dve.wait_ge(lg_ready, q + 1)
                dve.tensor_tensor(logits[:, C * (GATED + q):C * (GATED + q + 1), :],
                                  ps[:, 6 + q % 2, 0:C * E].rearrange("p (c e) -> p c e", c=C),
                                  across(gb[:, :], C), ALU.add).then_inc(lg_done, 1)
            rev = across(nums[:, 0:E], NT)

            def choose(values, top, into):
                step(dve.tensor_reduce(top[:, :], values[:, :, :], AX_X, ALU.max))
                step(dve.tensor_tensor(work[:, :, :], values[:, :, :], over(top[:, :], E), ALU.is_equal))
                step(dve.tensor_tensor(work[:, :, :], work[:, :, :], rev, ALU.mult))
                step(dve.tensor_reduce(pick[:, :], work[:, :, :], AX_X, ALU.max))
                step(dve.tensor_tensor(into[:, :, :], work[:, :, :], over(pick[:, :], E), ALU.is_equal))

            def route(c):
                if c == -1:
                    dve.wait_ge(consts_in, 16 * CONSTS)
                    dve.wait_ge(lg_done, Q)
                    choose(logits, best, first)
                    step(dve.scalar_tensor_tensor(both[:, :, :], first[:, :, :], -3.0e38, logits[:, :, :], ALU.mult, ALU.add))
                    choose(both, next_best, second)
                    step(dve.tensor_tensor(gap[:, :], next_best[:, :], best[:, :], ALU.subtract))
                    dve.tensor_tensor(both[:, :, :], first[:, :, :], second[:, :, :], ALU.add).then_inc(both_done, 1)
                    dve.sem_inc(gap_done, 1)
                elif c == 0:
                    step(dve.memset(zero[:, :], 0.0))
                    dve.wait_ge(ranks_ready, 1)
                    step(dve.tensor_copy(total[:, :, :], ps[:, RANKS, NT * E:2 * NT * E].rearrange("p (t e) -> p e t", e=E)))
                    step(dve.tensor_tensor_scan(upto[:, :, :].rearrange("p e t -> p (e t)"), total[:, :, :].rearrange("p e t -> p (e t)"),
                                                zero[:, :], 0.0, ALU.add, ALU.add))
                    step(dve.tensor_tensor(total[:, :, :], upto[:, :, :], total[:, :, :], ALU.subtract))
                    step(dve.tensor_tensor(count[:, :], upto[:, :, NT - 1], total[:, :, 0], ALU.subtract))
                    step(dve.tensor_scalar(tiles_i[:, :], count[:, :], float(TS - 1), None, ALU.add))
                    step(dve.tensor_scalar(tiles_i[:, :], tiles_i[:, :], TS.bit_length() - 1, None, ALU.arith_shift_right))
                    step(dve.tensor_copy(tiles_f[:, :], tiles_i[:, :]))
                    step(dve.tensor_tensor_scan(tiles_upto[:, :], tiles_f[:, :], zero[:, 0:E], 0.0, ALU.add, ALU.add))
                    step(dve.tensor_tensor(base[:, :], tiles_upto[:, :], tiles_f[:, :], ALU.subtract))
                    step(dve.scalar_tensor_tensor(base[:, :], base[:, :], float(TS), total[:, :, 0], ALU.mult, ALU.subtract))
                    step(dve.tensor_tensor(total[:, :, :], total[:, :, :], over(base[:, :], NT), ALU.add))
                    step(dve.tensor_tensor(work[:, :, :], ps[:, RANKS, 0:NT * E].rearrange("p (t e) -> p t e", e=E),
                                           total[:, :, :].rearrange("p e t -> p t e"), ALU.add))
                    for n, hot in enumerate((first, second)):
                        step(dve.tensor_tensor(hot[:, :, :], hot[:, :, :], work[:, :, :], ALU.mult))
                        step(dve.tensor_reduce(slotf[:, n, :], hot[:, :, :], AX_X, ALU.add))
                    step(dve.tensor_copy(slot[:, :, :], slotf[:, :, :]))
                    step(dve.tensor_tensor(passed[:, :, :], across(tiles_upto[:, :], TILES), over(nums[:, E:], E), ALU.is_le))
                    step(dve.tensor_reduce(owner[:, :], passed[:, :, :], AX_X, ALU.add))
                    dve.tensor_scalar(owner_i[:, :], owner[:, :], float(E - 1), None, ALU.min).then_inc(slots_known, 1)
                elif c == 6:
                    dve.wait_ge(gap_exp, 1)
                    step(dve.tensor_scalar(den[:, :], gap[:, :], 1.0, None, ALU.add))
                    step(dve.reciprocal(wt[:, 0, :], den[:, :]))
                    step(dve.tensor_tensor(wt[:, 1, :], gap[:, :], wt[:, 0, :], ALU.mult))

            route(-1)
            dve.wait_ge(first_w1_lo, HALF)
            dve.sem_inc(w_lo, HALF)
            for c in range(HALF, HC):
                split(dve, 0, 1, c, True)

            def turned(s, u):
                for k in range(DC):
                    dve.wait_ge(xhi_done, 2 * s + k + 1)
                    dve.tensor_tensor(xlo[:, u, k, :], ps[:, 6 + k, :], xhi[:, u, k, :].bitcast(F32), ALU.subtract).then_inc(xlo_done, 1)

            def halve(s, c):
                dve.wait_ge(gelu_done, HC * s + c + 1)
                if act_halves(s):
                    dve.wait_ge(last_hhi_done, HC * (s - LAST) + c + 1)
                else:
                    dve.tensor_copy(hhi[:, c % 2, :], h[:, c % 2, :]).then_inc(hhi_done, 1)
                    dve.wait_ge(hhi_done, HC * s + c + 1)
                dve.tensor_tensor(hlo[:, c % 2, :], h[:, c % 2, :], hhi[:, c % 2, :].bitcast(F32), ALU.subtract).then_inc(h_done, 1)

            def add_shared(s, u):
                t = tokens(s)
                if s < HEAD:
                    dve.wait_ge(sent[s % 2], GROUP * (s // 2 + 1))
                dve.wait_ge(ysum, (s if s < HEAD else s - TILES) + 1)
                dve.tensor_tensor(res[:, t[0]:t[-1] + 1, :], res[:, t[0]:t[-1] + 1, :], ys[:, u, :, :], ALU.add).then_inc(y_done, 1)

            def collect(s, u, w):
                dve.wait_ge(y_ready, s + 1)
                if not is_shared_now:
                    dve.wait_ge(y_out, 16 * (s - HEAD) + 16)
                for a in range(2):
                    ins = dve.tensor_tensor(ys[:, u, 2 * a:2 * a + 2, :],
                                            ps[:, 2 + 2 * u + a, :].rearrange("p (c d) -> p c d", c=2),
                                            bias2[:, w, :].unsqueeze(1).to_broadcast([P, 2, D]), ALU.add)
                if not is_shared_now:
                    ins.then_inc(y_done, 1)
                else:
                    ins.then_inc(ysum, 1)
                    if s:
                        add_shared(s, u)

            done = 0

            def mix(t):
                nonlocal done
                g = t % 4
                shared = t // C if t // C < HEAD else t // C + TILES
                dve.wait_ge(y_done, shared + 1)
                dve.wait_ge(back_in[g], 32 * (t // 4 + 1))
                for n in range(TOP):
                    dve.scalar_tensor_tensor(res[:, t, :], back[:, g, n, :], wt[:, n, t:t + 1], res[:, t, :],
                                             ALU.mult, ALU.add).then_inc(c_step, 1)
                    done += 1
                    dve.wait_ge(c_step, done)
                dve.bn_stats(bn[:, t % 2, :], res[:, t, :]).then_inc(c_step, 1)
                dve.wait_ge(c_step, done + 1)
                dve.bn_aggr(mv[:, t % 2, :], bn[:, t % 2, :]).then_inc(c_step, 1)
                done += 2
                dve.wait_ge(c_step, done)
                dve.tensor_scalar(var[:, t % 2:t % 2 + 1], mv[:, t % 2, 1:2], EPS, None, ALU.add).then_inc(var_done, 1)

            def finish(t):
                dve.wait_ge(rstd_done, t + 1)
                if t >= 4:
                    dve.wait_ge(fin_out[t % 4], 16 * (t // 4))
                dve.tensor_scalar(fin[:, t % 4, :], res[:, t, :], mv[:, t % 2, 0:1], rstd[:, t % 2:t % 2 + 1],
                                  ALU.subtract, ALU.mult).then_inc(fin_done, 1)

            def combine(n):
                if 0 <= n < NT:
                    mix(n)
                if 0 <= n - 1 < NT:
                    finish(n - 1)

            def tile(s, u, w, nxt=True, load=None, at=None, first_tiles=False):
                for c in range(HC):
                    if c < HC - 1:
                        halve(s, c + 1)
                    elif nxt:
                        halve(s + 1, 0)
                    if load is not None:
                        split(dve, load[0], load[1], c, True)
                    if first_tiles and s == 0:
                        route(c)
                    if first_tiles and s == 1 and c == 6:
                        add_shared(0, 0)
                    if c == 4 and nxt:
                        turned(s + 1, 1 - u)
                    if at is not None:
                        combine(at + c - LAG)
                collect(s, u, w)

            turned(0, 0)
            halve(0, 0)
            is_shared_now = True
            for s in range(HEAD):
                tile(s, s % 2, 1, True, (1, 0) if s == HEAD - 1 else None, first_tiles=True)
            is_shared_now = False
            with dve.Fori(0, (TILES - 1) // 2) as i:
                for u in range(2):
                    tile(HEAD + 2 * i + u, u, u, True, (2 * i + u + 2, 1 - u))
            tile(LAST - 1, 0, 0, True, (TILES + 1, 1))
            is_shared_now = True
            for s in range(LAST, END):
                tile(s, s % 2, 1, s < END - 1, None, HC * (s - LAST))
            for n in range(HC * LASTS - LAG, NT + 1):
                combine(n)


def host_constants():
    inv = np.float32(10000.0) ** (-np.arange(0, DR, 2, dtype=np.float32) / np.float32(DR))
    ang = np.arange(S, dtype=np.float32)[:, None] * inv
    rope = np.zeros((P, 2, S), np.float32)
    rope[:, 0, :] = 1.0
    for i in range(HG):
        for r in range(DR):
            row = SLOT * i + DH + r
            rope[row, 0] = np.cos(ang[:, r // 2])
            rope[row, 1] = np.sin(ang[:, r // 2]) * (-1.0 if r % 2 == 0 else 1.0)
    masks = np.zeros((P, 5, P), np.float32)
    for i in range(HG):
        for d in range(DH):
            masks[SLOT * i + d, 0, DH * i + d] = 1.0
        masks[SLOT * i + DH, 0, HG * DH + i] = 1.0
    masks[:, 1, :] = np.eye(P)
    masks[:, 2, :] = np.triu(np.ones((P, P)), 1)
    masks[:, 3, :] = 1.0
    masks[:, 4, :] = np.triu(np.ones((P, P)))
    numbers = np.zeros((P, E + TILES), np.float32)
    numbers[:, :E] = E - np.arange(E)
    numbers[:, E:] = np.arange(TILES)
    return rope, masks, numbers


def attention_layouts(x, W_DQ, W_UQ, W_QR, W_DKV, W_UK, W_UV, W_KR, W_O):
    xf = x.reshape(T, D)
    x_tok = np.ascontiguousarray(xf.reshape(NT, P, D).transpose(1, 0, 2))
    x_t = np.ascontiguousarray(xf.T.reshape(DC, P, T).transpose(1, 0, 2))
    w_down = np.concatenate([W_DQ, W_DKV], axis=1).reshape(DC, P, 2 * LAT).transpose(1, 0, 2)
    partner = np.arange(DR) ^ 1
    w_q = np.zeros((LAT, 2, H, SLOT), np.float32)
    w_q[:, 0, :, :DH] = W_UQ.reshape(LAT, H, DH)
    w_q[:, 0, :, DH:DH + DR] = W_QR.reshape(LAT, H, DR)
    w_q[:, 1, :, DH:DH + DR] = W_QR.reshape(LAT, H, DR)[:, :, partner]
    w_q = w_q.reshape(LAT, 2, G, P).transpose(0, 2, 1, 3)
    w_k = np.zeros((LAT, H, SLOT), np.float32)
    w_k[:, :, :DH] = W_UK.reshape(LAT, H, DH)
    w_kv = np.concatenate([w_k.reshape(LAT, G * P), W_UV], axis=1)
    w_kr = np.zeros((D, 2, HG, SLOT), np.float32)
    w_kr[:, 0, :, DH:DH + DR] = W_KR[:, None, :]
    w_kr[:, 1, :, DH:DH + DR] = W_KR[:, None, partner]
    w_kr = w_kr.reshape(DC, P, 2, P).transpose(1, 0, 2, 3)
    w_o = W_O.reshape(DC, P, D).transpose(1, 0, 2)
    return [np.ascontiguousarray(a) for a in (x_tok, x_t, w_down, w_q, w_kv, w_kr, w_o)]


def build(nc, x, xT, w_down, w_q, w_kv, w_kr, w_o, w1, w2, b1, b2, gate_w, gate_b, rope, masks, numbers, out):
    slots_in = nc.dram_tensor("slots_in", (SLOTS, D), F32, kind="Internal").ap()
    slots_out = nc.dram_tensor("slots_out", (SLOTS, D), F32, kind="Internal").ap()
    with (nc.sbuf_tensor("res", [P, NT, D], F32) as res, nc.sbuf_tensor("logits", [P, NT, E], F32) as logits,
          nc.sbuf_tensor("ident", [P, P], F32) as ident,
          nc.sbuf_tensor("gw", [P, DC, E], F32) as gw, nc.sbuf_tensor("gb", [P, E], F32) as gb):
        attention(nc, x, xT, w_down, w_q, w_kv, w_kr, w_o, rope, masks, gate_w, gate_b, res, ident, gw, gb, logits,
                  slots_in)
        experts(nc, res, ident, gw, gb, logits, slots_in, slots_out, w1, w2, b1, b2, masks, numbers, out)


_INS = ["x", "xT", "w_down", "w_q", "w_kv", "w_kr", "w_o", "w1", "w2", "b1", "b2", "gate_w", "gate_b",
        "rope", "masks", "numbers"]


def kernel(L0_attn_x, L0_attn_W_DQ, L0_attn_W_UQ, L0_attn_W_QR, L0_attn_W_DKV, L0_attn_W_UK, L0_attn_W_UV,
           L0_attn_W_KR, L0_attn_W_O, L0_ffn_gate_w, L0_ffn_gate_b, L0_ffn_w1, L0_ffn_b1, L0_ffn_w2, L0_ffn_b2,
           L0_ffn_ws1, L0_ffn_bs1, L0_ffn_ws2, L0_ffn_bs2):
    import concourse.bacc as bacc
    from concourse.bass_utils import run_bass_kernel_spmd

    a = lambda v: np.asarray(v)
    laid = attention_layouts(a(L0_attn_x), a(L0_attn_W_DQ), a(L0_attn_W_UQ), a(L0_attn_W_QR), a(L0_attn_W_DKV),
                             a(L0_attn_W_UK), a(L0_attn_W_UV), a(L0_attn_W_KR), a(L0_attn_W_O))
    w1 = np.concatenate([a(L0_ffn_w1), a(L0_ffn_ws1)[None]])
    w2 = np.concatenate([a(L0_ffn_w2), a(L0_ffn_ws2)[None]])
    b1 = np.concatenate([a(L0_ffn_b1), a(L0_ffn_bs1)[None]]).reshape(E + 1, HID // P, P).transpose(0, 2, 1)
    b2 = np.concatenate([a(L0_ffn_b2), a(L0_ffn_bs2)[None]])
    arrays = dict(zip(_INS, laid + [w1, w2, b1, b2, a(L0_ffn_gate_w), a(L0_ffn_gate_b), *host_constants()]))
    arrays = {n: np.ascontiguousarray(v) for n, v in arrays.items()}
    nc = bacc.Bacc("TRN2", target_bir_lowering=False, num_devices=1)
    aps = [nc.dram_tensor(n, v.shape, mybir.dt.from_np(v.dtype), kind="ExternalInput").ap() for n, v in arrays.items()]
    out = nc.dram_tensor("out", (T, D), F32, kind="ExternalOutput").ap()
    build(nc, *aps, out)
    r = run_bass_kernel_spmd(nc, [arrays], core_ids=[0])
    return r.results[0]["out"].reshape(B, S, D)
```
